# Optimizing a Trainium2 kernel written in Bass

```python
import numpy as np
import jax
import jax.numpy as jnp

def _softmax(x, axis=-1):
    return jax.nn.softmax(x, axis=axis)

def _gelu(x):
    return jax.nn.gelu(x, approximate=True)

def _silu(x):
    return jax.nn.silu(x)

def _sigmoid(x):
    return jax.nn.sigmoid(x)

def _layernorm(x, axis=-1, eps=1e-05):
    m = jnp.mean(x, axis=axis, keepdims=True)
    v = jnp.var(x, axis=axis, keepdims=True)
    return (x - m) / jnp.sqrt(v + eps)

def _scatter_add(tgt, idx, src, axis=0):
    return tgt.at[idx].add(src)

def _segment_sum(src, seg, n):
    return jax.ops.segment_sum(src, seg, n)
kernel_name = 'mk_gnn_preln_d1_gnn_r8_9f6caf'

def setup_inputs(seed: int=0):
    np.random.seed(seed)
    _w = jnp.asarray

    def _rec_inputs():
        import jax
        import jax.numpy as jnp
        _gk = jax.random.key(seed)
        x = -0.0005121 + 1.001 * jax.random.normal(jax.random.fold_in(_gk, 1), (6250, 64), jnp.float32)
        src = jax.random.randint(jax.random.fold_in(_gk, 2), (200000,), 0, 6250, jnp.int32)
        dst = jnp.minimum((6250 * jax.random.uniform(jax.random.fold_in(_gk, 3), (200000,)) ** 2.0).astype(jnp.int32), 49999)
        _o = jnp.argsort(dst, stable=True)
        src = src[_o]
        dst = dst[_o]
        edge_attr_16 = 0.000714719 + 1.00021 * jax.random.normal(jax.random.fold_in(_gk, 11), (200000, 16), jnp.float32)
        return (x, src, dst, edge_attr_16)
    x, src, dst, edge_attr_16 = _rec_inputs()

    def _L0_gnn_setup():
        import jax, jax.numpy as jnp
        import numpy as np
        N_NODES = 6250
        N_EDGES = 25000
        NODE_F = 64
        EDGE_F = 16
        HID = 32
        LAT = 16

        def _glorot(key, shape):
            fan_in, fan_out = (shape[0], shape[1])
            lim = np.sqrt(6.0 / (fan_in + fan_out))
            return jax.random.uniform(key, shape, jnp.float32, -lim, lim)

        def _nnconv(x, src, dst, edge_attr, w1, b1, w2, b2, root_w, root_b):
            h = jax.nn.relu(edge_attr @ w1 + b1)
            w_e = (h @ w2 + b2).reshape(-1, HID, HID)
            msg = jnp.einsum('eh,eho->eo', x[src], w_e)
            agg = jax.ops.segment_sum(msg, dst, num_segments=N_NODES)
            cnt = jax.ops.segment_sum(jnp.ones((msg.shape[0], 1), x.dtype), dst, num_segments=N_NODES)
            agg = agg / jnp.maximum(cnt, 1.0)
            return agg + x @ root_w + root_b
        key = jax.random.key(seed)
        ks = jax.random.split(key, 24)
        inp = {'x': jax.random.normal(ks[0], (N_NODES, NODE_F), jnp.float32), 'edge_index': jax.random.randint(ks[1], (2, N_EDGES), 0, N_NODES, jnp.int64), 'edge_attr': jax.random.normal(ks[2], (N_EDGES, EDGE_F), jnp.float32), 'lin_in_w': _glorot(ks[3], (NODE_F, HID)), 'lin_in_b': jnp.zeros((HID,), jnp.float32), 'edge_w1': jnp.stack([_glorot(ks[4 + i], (EDGE_F, HID)) for i in range(3)]), 'edge_b1': jnp.zeros((3, HID), jnp.float32), 'edge_w2': jnp.stack([_glorot(ks[7 + i], (HID, HID * HID)) * 0.1 for i in range(3)]), 'edge_b2': jnp.zeros((3, HID * HID), jnp.float32), 'root_w': jnp.stack([_glorot(ks[10 + i], (HID, HID)) for i in range(3)]), 'root_b': jnp.zeros((3, HID), jnp.float32), 'lin_out_w': _glorot(ks[13], (HID, LAT)), 'lin_out_b': jnp.zeros((LAT,), jnp.float32), 'dec_w1': _glorot(ks[14], (LAT, HID)), 'dec_b1': jnp.zeros((HID,), jnp.float32), 'dec_w2': _glorot(ks[15], (HID, NODE_F)), 'dec_b2': jnp.zeros((NODE_F,), jnp.float32)}
        return inp
    _L0_gnn_all = _L0_gnn_setup()
    _L0_gnn_in = {k: v for k, v in _L0_gnn_all.items() if k in ('lin_in_w', 'lin_in_b', 'edge_w1', 'edge_b1', 'edge_w2', 'edge_b2', 'root_w', 'root_b', 'lin_out_w', 'lin_out_b', 'dec_w1', 'dec_b1', 'dec_w2', 'dec_b2')}
    del _L0_gnn_all
    return {'x': x, 'src': src, 'dst': dst, 'edge_attr_16': edge_attr_16, 'L0_gnn_lin_in_w': _L0_gnn_in['lin_in_w'], 'L0_gnn_lin_in_b': _L0_gnn_in['lin_in_b'], 'L0_gnn_edge_w1': _L0_gnn_in['edge_w1'], 'L0_gnn_edge_b1': _L0_gnn_in['edge_b1'], 'L0_gnn_edge_w2': _L0_gnn_in['edge_w2'], 'L0_gnn_edge_b2': _L0_gnn_in['edge_b2'], 'L0_gnn_root_w': _L0_gnn_in['root_w'], 'L0_gnn_root_b': _L0_gnn_in['root_b'], 'L0_gnn_lin_out_w': _L0_gnn_in['lin_out_w'], 'L0_gnn_lin_out_b': _L0_gnn_in['lin_out_b'], 'L0_gnn_dec_w1': _L0_gnn_in['dec_w1'], 'L0_gnn_dec_b1': _L0_gnn_in['dec_b1'], 'L0_gnn_dec_w2': _L0_gnn_in['dec_w2'], 'L0_gnn_dec_b2': _L0_gnn_in['dec_b2']}

def reference(x, src, dst, edge_attr_16, L0_gnn_lin_in_w, L0_gnn_lin_in_b, L0_gnn_edge_w1, L0_gnn_edge_b1, L0_gnn_edge_w2, L0_gnn_edge_b2, L0_gnn_root_w, L0_gnn_root_b, L0_gnn_lin_out_w, L0_gnn_lin_out_b, L0_gnn_dec_w1, L0_gnn_dec_b1, L0_gnn_dec_w2, L0_gnn_dec_b2):
    import jax
    import jax.numpy as jnp

    def _L0_gnn_ref(x, edge_index, edge_attr, lin_in_w, lin_in_b, edge_w1, edge_b1, edge_w2, edge_b2, root_w, root_b, lin_out_w, lin_out_b, dec_w1, dec_b1, dec_w2, dec_b2):
        import jax, jax.numpy as jnp
        import numpy as np
        N_NODES = 6250
        N_EDGES = 25000
        NODE_F = 64
        EDGE_F = 16
        HID = 32
        LAT = 16

        def _glorot(key, shape):
            fan_in, fan_out = (shape[0], shape[1])
            lim = np.sqrt(6.0 / (fan_in + fan_out))
            return jax.random.uniform(key, shape, jnp.float32, -lim, lim)

        def _nnconv(x, src, dst, edge_attr, w1, b1, w2, b2, root_w, root_b):
            h = jax.nn.relu(edge_attr @ w1 + b1)
            w_e = (h @ w2 + b2).reshape(-1, HID, HID)
            msg = jnp.einsum('eh,eho->eo', x[src], w_e)
            agg = jax.ops.segment_sum(msg, dst, num_segments=N_NODES)
            cnt = jax.ops.segment_sum(jnp.ones((msg.shape[0], 1), x.dtype), dst, num_segments=N_NODES)
            agg = agg / jnp.maximum(cnt, 1.0)
            return agg + x @ root_w + root_b
        src, dst = (edge_index[0], edge_index[1])
        h = jax.nn.relu(x @ lin_in_w + lin_in_b)
        for i in range(3):
            h = _nnconv(h, src, dst, edge_attr, edge_w1[i], edge_b1[i], edge_w2[i], edge_b2[i], root_w[i], root_b[i])
            h = jax.nn.relu(h)
        z = h @ lin_out_w + lin_out_b
        d = jax.nn.relu(z @ dec_w1 + dec_b1)
        return d @ dec_w2 + dec_b2
    edge_index = jnp.stack([src, dst])
    h = jnp.maximum(_layernorm(x, axis=-1), 0.0)
    x = x + _L0_gnn_ref(h, edge_index, edge_attr_16, L0_gnn_lin_in_w, L0_gnn_lin_in_b, L0_gnn_edge_w1, L0_gnn_edge_b1, L0_gnn_edge_w2, L0_gnn_edge_b2, L0_gnn_root_w, L0_gnn_root_b, L0_gnn_lin_out_w, L0_gnn_lin_out_b, L0_gnn_dec_w1, L0_gnn_dec_b1, L0_gnn_dec_w2, L0_gnn_dec_b2)
    return x

_drawn_inputs = setup_inputs


def setup_inputs(seed=0):
    import zlib

    import numpy as np

    out = dict(_drawn_inputs(seed))
    spreads = {'L0_gnn_lin_in_b': (0.0, 0.598),
     'L0_gnn_edge_b1': (0.0, 2.0),
     'L0_gnn_edge_b2': (0.0, 0.1),
     'L0_gnn_root_b': (0.0, 0.8),
     'L0_gnn_lin_out_b': (0.0, 2.0),
     'L0_gnn_dec_b1': (0.0, 0.8),
     'L0_gnn_dec_b2': (0.0, 0.8)}
    factors = {'edge_attr_16': 8.0, 'L0_gnn_edge_w1': 8.0, 'L0_gnn_edge_w2': 5.675}
    for name, (base, spread) in spreads.items():
        noise = np.random.default_rng([zlib.crc32(name.encode()), seed]).standard_normal(out[name].shape)
        drawn = base * np.exp(spread * noise) if base else spread * noise
        out[name] = jnp.asarray(drawn.astype(out[name].dtype))
    for name, factor in factors.items():
        out[name] = (out[name] * factor).astype(out[name].dtype)
    return out
```

```python
from contextlib import ExitStack

import concourse.bass as bass
from concourse import mybir

F32 = mybir.dt.float32
BF16 = mybir.dt.bfloat16
I32 = mybir.dt.int32
U32 = mybir.dt.uint32
ALU = mybir.AluOpType
ACT = mybir.ActivationFunctionType
AX = mybir.AxisListType

P = 128
N_NODES = 6250
N_EDGES = 200000
NODE_F = 64
EDGE_F = 16
HID = 32
LAT = 16
LAYERS = 3
EPS = 1e-5

JN = P // HID
GROUPS = -(-N_NODES // JN)
ROWS = -(-GROUPS // P)
GPAD = ROWS * P
GBANK = -(-GROUPS // 4)
GBANKS = [(b * GBANK, min(GBANK, GROUPS - b * GBANK)) for b in range(4)]

SUB = 6
SUBS = 3
SEG = SUB * SUBS
SEGS = 3
CHUNK = SEG * SEGS
CHUNKS = -(-N_EDGES // (P * CHUNK))
TILES = CHUNKS * CHUNK
TROWS = -(-TILES // P)
TPAD = TROWS * P
RING = 3
GRING = SEGS * SUBS
HE_SEGS = CHUNKS * SEGS + 2

WINDOWS = [(0, 9, 2), (9, 18, 3), (18, CHUNKS, 4)]
NGMAX = 4
WMAX = JN * NGMAX
K1 = HID + 1
PARTS = 3
PW = HID // 2
ROW_W = PARTS * PW
FAR = 1 << 20
LCM = 12
PRODUCTS = [(0, 0), (0, 1), (1, 0), (1, 1), (0, 2), (2, 0)]


def groups_of_tile(t):
    c = min(t // CHUNK, CHUNKS - 1)
    return next(ng for a, b, ng in WINDOWS if a <= c < b)


def gnn_program(nc, x_rows, src_t, dst_t, ea_t, w1_b, w2_b, root_b, root_bias, lin_w, lin_bias,
                lout_b, lout_bias, dec1_b, dec1_bias, dec2_b, dec2_bias, tile_ng, tile_valid,
                tile_scale, out):
    table = nc.dram_tensor("node_table", (GPAD * JN, ROW_W), U32, kind="Internal").ap()
    local_dram = nc.dram_tensor("local_of_edge", (P, TPAD), F32, kind="Internal").ap()
    table_rows = table.rearrange("(c p j) w -> p c (j w)", p=P, j=JN)

    with ExitStack() as ctx:
        def sb(name, shape, dt=F32):
            return ctx.enter_context(nc.sbuf_tensor(name, shape, dt))

        sem_list = []

        def sem(name):
            s = ctx.enter_context(nc.semaphore(name))
            sem_list.append(s)
            return s

        ps = ctx.enter_context(nc.psum_tensor("ps", [P, 8, 512], F32))

        ident = sb("ident", [P, P])
        node_h = sb("node_h", [P, GPAD])
        agg = sb("agg", [P, GROUPS])
        recip = sb("recip", [P, GROUPS])
        iota_g = sb("iota_g", [P, NGMAX - 1 + GROUPS])
        iota_w = sb("iota_w", [P, WMAX])
        local = sb("local", [P, TPAD])
        g0_first = sb("g0_first", [P, TROWS])
        g0 = sb("g0", [P, TROWS])
        g0_next = sb("g0_next", [P, TROWS])
        ngt = sb("ngt", [P, TROWS])
        ngt4 = sb("ngt4", [P, TROWS])
        passes_i = sb("passes_i", [1, 1], I32)
        msg_t = sb("msg_t", [P, NGMAX, TPAD])
        onehot = sb("onehot", [P, 2, NGMAX - 1 + GROUPS + 1], BF16)
        w2 = sb("w2", [P, K1, P])
        w1 = sb("w1", [SUB * EDGE_F + 1, SUB * HID])
        rootw = sb("rootw", [P, P])
        rootbias = sb("rootbias", [P, 1])
        ea = sb("ea", [SUB * EDGE_F + 1, RING, SUBS, P])
        idx = sb("idx", [P, RING, SEG], U32)
        xg = sb("xg", [P, GRING, SUB, ROW_W], U32)
        eq = sb("eq", [P, SEG, WMAX], I32)
        mask = sb("mask", [P, RING, SEG, WMAX], I32)
        he32 = sb("he32", [P, RING, SEG, HID])
        he_r = sb("he_r", [P, SEG, HID])
        hp = sb("hp", [P, RING, PARTS, SEG, K1], BF16)

        XM_W = PARTS * SUB * WMAX * PW
        work = sb("work", [P, RING * XM_W])
        xm = work[:, :].bitcast(U32).rearrange("p (s w) -> p s w", s=RING)
        mk = sb("mk", [P, K1, CHUNK * NGMAX])
        mk_flat = mk[:, :, :].rearrange("p k u -> p (k u)")

        XW = ROWS * JN * NODE_F
        x_in = work[:, 0:XW]
        x_c = work[:, XW:2 * XW]
        x_s = work[:, 2 * XW:3 * XW]
        x_t = work[:, 3 * XW:4 * XW].rearrange("p (a g) -> p a g", a=2)
        LT_W = TROWS * P
        loc_t = mk_flat[:, 0:LT_W].rearrange("p (c e) -> p c e", c=TROWS)
        dst_i = mk_flat[:, LT_W:2 * LT_W].bitcast(I32)
        dst_f = mk_flat[:, 2 * LT_W:3 * LT_W]
        dst_m = work[:, 0:LT_W]
        cmp = work[:, 0:WMAX * P].rearrange("p (w e) -> p w e", w=WMAX)
        cnt = work[:, WMAX * P:WMAX * P + TROWS * WMAX].rearrange("p (c w) -> p c w", c=TROWS)
        cnt_b = work[:, 3400:3400 + WMAX * HID].bitcast(BF16).rearrange("p (d w) -> p d w", d=2)
        valid = work[:, 3072:3072 + TROWS * WMAX].rearrange("p (c w) -> p c w", c=TROWS)
        he_ps = ps[:, 6:8, :].rearrange("p b c -> p (b c)").rearrange("p (a c) -> p a c", a=4)[:, 0:SUBS, :]
        contr = ps[:, 7, 256:512]
        r_parts = work[:, 0:2 * PARTS * 256].bitcast(BF16).rearrange("p (d a w) -> p d a w", d=2, a=PARTS)
        r_rest = work[:, 2 * PARTS * 256:2 * PARTS * 256 + 1024].rearrange("p (d w) -> p d w", d=2)
        small = sb("small", [P, 8, ROWS * JN])
        prew = sb("prew", [P, 2, P])
        biases = sb("biases", [P, 4])
        iota_i = mk_flat[:, 3 * LT_W:3 * LT_W + NGMAX - 1 + GROUPS].bitcast(I32)

        s_load = sem("s_load")
        s_w = sem("s_w")
        s_dve = sem("s_dve")
        s_act = sem("s_act")
        s_pe = sem("s_pe")
        s_pool = sem("s_pool")
        s_store = sem("s_store")
        idx_in = [sem(f"idx_in{i}") for i in range(RING)]
        ea_in = [sem(f"ea_in{i}") for i in range(RING)]
        gathered = [sem(f"gathered{i}") for i in range(GRING)]
        slot_taken = sem("slot_taken")
        mask_eq = sem("mask_eq")
        mask_set = sem("mask_set")
        xm_done = sem("xm_done")
        units_done = sem("units_done")
        he_mm = sem("he_mm")
        he_act = sem("he_act")
        he_r1 = sem("he_r1")
        he_mid = sem("he_mid")
        he_split = sem("he_split")
        evac = sem("evac")
        contr_done = sem("contr_done")
        r_done = sem("r_done")

        def stage_end():
            nums = [s.num for s in sem_list]
            assert max(nums) - min(nums) == len(nums) - 1
            nc.gpsimd.dma_reset(range(min(nums), max(nums) + 1))
            nc.gpsimd.sem_clear(range(min(nums), max(nums) + 1))
            nc.all_engine_barrier(sem_only=True)

        with nc.Block() as block:
            @block.sync
            def _(sp):
                sp.dma_start(dst_i, dst_t).then_inc(s_load, 16)
                sp.dma_start(ngt[:, :], tile_ng).then_inc(s_load, 16)
                sp.dma_start(small[:, 7, 0:TROWS], tile_scale).then_inc(s_load, 16)
                sp.dma_start(prew[:, :, :], lin_w).then_inc(s_w, 16)
                sp.dma_start(biases[:, 0:1], lin_bias).then_inc(s_w, 16)
                sp.wait_ge(s_dve, 4)
                sp.dma_start(x_in.rearrange("p (c w) -> p c w", c=ROWS), x_rows).then_inc(s_w, 16)
                sp.wait_ge(s_act, TROWS)
                sp.dma_start(local_dram, local[:, :]).then_inc(s_store, 16)
                sp.wait_ge(s_store, 16)

            @block.gpsimd
            def _(pool):
                nc.gpsimd.memset(ident[:, :], 0.0).then_inc(s_pool, 1)
                nc.gpsimd.iota(iota_i, pattern=[[1, NGMAX - 1 + GROUPS]], base=-(NGMAX - 1),
                               channel_multiplier=0).then_inc(s_pool, 1)
                pool.wait_ge(s_pool, 2)
                nc.gpsimd.affine_select(out=ident[:, :], in_=ident[:, :], compare_op=ALU.not_equal, fill=1.0,
                                        base=0, pattern=[[-1, P]], channel_multiplier=1).then_inc(s_pool, 1)
                pool.wait_ge(s_pool, 3)
                nc.gpsimd.memset(msg_t[:, :, :], 0.0)
                nc.gpsimd.memset(hp[:, :, :, :, :], 0.0).then_inc(s_pool, 1)
                pool.wait_ge(s_pool, 4)
                nc.gpsimd.memset(hp[:, :, 0, :, HID:K1], 1.0).then_inc(s_pool, 1)
                pool.wait_ge(s_dve, 8)
                nc.gpsimd.partition_all_reduce(small[:, 6, 2:3], small[:, 6, 1:2], P,
                                               bass.bass_isa.ReduceOp.max).then_inc(s_pool, 1)

            @block.vector
            def _(dve):
                nc.vector.memset(ea[SUB * EDGE_F:SUB * EDGE_F + 1, :, :, :], 1.0)
                dve.wait_ge(s_load, 48)
                nc.vector.tensor_scalar(ngt4[:, :], ngt[:, :], float(JN), None, ALU.mult)
                nc.vector.tensor_copy(dst_f, dst_i).then_inc(s_dve, 1)
                dve.wait_ge(s_dve, 1)
                nc.vector.tensor_scalar(dst_m, dst_f, 0.0, float(FAR), ALU.is_lt, ALU.mult).then_inc(s_dve, 1)
                dve.wait_ge(s_dve, 2)
                nc.vector.tensor_tensor(dst_m, dst_m, dst_f, ALU.add).then_inc(s_dve, 1)
                dve.wait_ge(s_dve, 3)
                nc.vector.tensor_reduce(small[:, 0, 0:TROWS], dst_m.rearrange("p (c e) -> p c e", c=TROWS),
                                        axis=AX.X, op=ALU.min)
                nc.vector.tensor_reduce(small[:, 1, 0:TROWS], dst_f.rearrange("p (c e) -> p c e", c=TROWS),
                                        axis=AX.X, op=ALU.max).then_inc(s_dve, 1)
                dve.wait_ge(s_dve, 4)
                lo_i = small[:, 2, 0:TROWS].bitcast(I32)
                hi_i = small[:, 3, 0:TROWS].bitcast(I32)
                nc.vector.tensor_copy(lo_i, small[:, 0, 0:TROWS])
                nc.vector.tensor_copy(hi_i, small[:, 1, 0:TROWS]).then_inc(s_dve, 1)
                dve.wait_ge(s_dve, 5)
                lo_g = small[:, 4, 0:TROWS].bitcast(I32)
                hi_g = small[:, 5, 0:TROWS].bitcast(I32)
                nc.vector.tensor_scalar(lo_g, lo_i, 2, None, ALU.arith_shift_right)
                nc.vector.tensor_scalar(hi_g, hi_i, 2, None, ALU.arith_shift_right).then_inc(s_dve, 1)
                dve.wait_ge(s_dve, 6)
                nc.vector.tensor_copy(g0_first[:, :], lo_g)
                nc.vector.tensor_copy(small[:, 0, 0:TROWS], hi_g).then_inc(s_dve, 1)
                dve.wait_ge(s_dve, 7)
                nc.vector.tensor_tensor(small[:, 1, 0:TROWS], small[:, 0, 0:TROWS], g0_first[:, :], ALU.subtract)
                nc.vector.tensor_scalar(small[:, 2, 0:TROWS], g0_first[:, :], float(JN), None, ALU.mult)
                nc.vector.drain()
                nc.vector.scalar_tensor_tensor(small[:, 3, 0:TROWS], small[:, 1, 0:TROWS], 1.0,
                                               small[:, 7, 0:TROWS], ALU.add, ALU.mult)
                nc.vector.drain()
                nc.vector.tensor_reduce(small[:, 6, 1:2], small[:, 3, 0:TROWS], axis=AX.X,
                                        op=ALU.max).then_inc(s_dve, 1)
                nc.vector.tensor_tensor(loc_t, dst_f.rearrange("p (c e) -> p c e", c=TROWS),
                                        small[:, 2, 0:TROWS].unsqueeze(2).to_broadcast([P, TROWS, P]),
                                        ALU.subtract).then_inc(s_dve, 1)
                dve.wait_ge(s_pool, 5)
                nc.vector.tensor_copy(iota_g[:, :], iota_i).then_inc(s_dve, 1)
                dve.wait_ge(s_dve, 10)
                nc.vector.tensor_scalar(iota_w[:, :], iota_g[:, NGMAX - 1:NGMAX - 1 + WMAX], 0.0, None, ALU.add)
                dve.wait_ge(s_pool, 6)
                nc.vector.tensor_copy(passes_i[0:1, 0:1], small[0:1, 6, 2:3]).then_inc(s_dve, 1)

                dve.wait_ge(s_w, 48)
                x3 = x_in.rearrange("p (n f) -> p n f", f=NODE_F)
                c3 = x_c.rearrange("p (n f) -> p n f", f=NODE_F)
                s3 = x_s.rearrange("p (n f) -> p n f", f=NODE_F)
                nn = [P, ROWS * JN, NODE_F]
                nc.vector.tensor_reduce(small[:, 0, :], x3, axis=AX.X, op=ALU.add)
                nc.vector.drain()
                nc.vector.tensor_scalar(small[:, 1, :], small[:, 0, :], 1.0 / NODE_F, None, ALU.mult)
                nc.vector.drain()
                nc.vector.tensor_tensor(c3, x3, small[:, 1, :].unsqueeze(2).to_broadcast(nn), ALU.subtract)
                nc.vector.drain()
                nc.vector.tensor_tensor(x_s, x_c, x_c, ALU.mult)
                nc.vector.drain()
                nc.vector.tensor_reduce(small[:, 2, :], s3, axis=AX.X, op=ALU.add)
                nc.vector.drain()
                nc.vector.tensor_scalar(small[:, 3, :], small[:, 2, :], 1.0 / NODE_F, EPS, ALU.mult,
                                        ALU.add).then_inc(s_dve, 1)
                dve.wait_ge(s_act, TROWS + 1)
                nc.vector.reciprocal(small[:, 5, :], small[:, 4, :])
                nc.vector.drain()
                nc.vector.tensor_tensor(s3, c3, small[:, 5, :].unsqueeze(2).to_broadcast(nn), ALU.mult)
                nc.vector.drain()
                nc.vector.tensor_scalar(x_c, x_s, 0.0, None, ALU.max).then_inc(s_dve, 1)

            @block.tensor
            def _(pe):
                pe.wait_ge(s_dve, 9)
                pe.wait_ge(s_pool, 3)
                for c in range(TROWS):
                    if c >= 4:
                        pe.wait_ge(s_act, c - 3)
                    nc.tensor.transpose(ps[:, c % 4, 0:P], loc_t[:, c, :], ident[:, :]).then_inc(s_pe, 1)
                pe.wait_ge(s_dve, 13)
                for a in range(2):
                    for c in range(ROWS):
                        n = a * ROWS + c
                        if n >= 4:
                            pe.wait_ge(s_act, TROWS + 1 + n - 3)
                        nc.tensor.transpose(ps[:, 4 + n % 4, 0:P],
                                            x_c[:, (2 * c + a) * P:(2 * c + a + 1) * P],
                                            ident[:, :]).then_inc(s_pe, 1)
                pe.wait_ge(s_act, TROWS + 1 + 2 * ROWS)
                pe.wait_ge(s_w, 48)
                for b in range(4):
                    w = GPAD // 4
                    for a in range(2):
                        last = nc.tensor.matmul(ps[:, b, 0:w], prew[:, a, :], x_t[:, a, b * w:(b + 1) * w],
                                                start=(a == 0), stop=(a == 1))
                    last.then_inc(s_pe, 1)

            @block.scalar
            def _(act):
                for c in range(TROWS):
                    act.wait_ge(s_pe, c + 1)
                    nc.scalar.copy(local[:, c * P:(c + 1) * P], ps[:, c % 4, 0:P]).then_inc(s_act, 1)
                act.wait_ge(s_dve, 12)
                nc.scalar.activation(small[:, 4, :], small[:, 3, :], ACT.Sqrt).then_inc(s_act, 1)
                for n in range(2 * ROWS):
                    act.wait_ge(s_pe, TROWS + n + 1)
                    nc.scalar.copy(x_t[:, n // ROWS, (n % ROWS) * P:(n % ROWS + 1) * P],
                                   ps[:, 4 + n % 4, 0:P]).then_inc(s_act, 1)
                act.wait_ge(s_w, 48)
                for b in range(4):
                    w = GPAD // 4
                    act.wait_ge(s_pe, TROWS + 2 * ROWS + b + 1)
                    nc.scalar.activation(node_h[:, b * w:(b + 1) * w], ps[:, b, 0:w], ACT.Relu,
                                         bias=biases[:, 0:1]).then_inc(s_act, 1)
        stage_end()

        need = nc.values_load(passes_i[0:1, 0:1], min_val=1, max_val=LCM * GROUPS)
        n_passes = (need + (LCM - 1)) // LCM

        def group_products(terms, c):
            for b, (g_at, g_n) in enumerate(GBANKS):
                for n, (g, sums) in enumerate(terms):
                    at = NGMAX - 1 - g + g_at
                    last = nc.tensor.matmul(ps[:, b, 0:g_n], sums, onehot[:, c % 2, at:at + g_n],
                                            start=c == 0 and n == 0,
                                            stop=c == TROWS - 1 and n == len(terms) - 1)
            return last

        with nc.Block() as block:
            @block.sync
            def _(sp):
                sp.dma_start(valid.rearrange("p c w -> p (c w)"), tile_valid).then_inc(s_load, 16)

            @block.vector
            def _(dve):
                nc.vector.memset(recip[:, :], 0.0)
                nc.vector.tensor_copy(g0[:, :], g0_first[:, :]).then_inc(s_dve, 1)
                dve.wait_ge(s_load, 16)
        stage_end()
        with nc.Fori(0, n_passes) as _p:
            with nc.Block() as block:
                @block.vector
                def _(dve):
                    for c in range(TROWS):
                        nc.vector.tensor_tensor(cmp, loc_t[:, c, :].unsqueeze(1).to_broadcast([P, WMAX, P]),
                                                iota_w[:, :].unsqueeze(2).to_broadcast([P, WMAX, P]),
                                                ALU.is_equal)
                        nc.vector.drain()
                        nc.vector.tensor_reduce(cnt[:, c, :], cmp, axis=AX.X, op=ALU.add)
                        nc.vector.drain()
                    nc.vector.tensor_tensor(cnt, cnt, valid, ALU.mult)
                    nc.vector.drain()
                    for c in range(TROWS):
                        if c >= 2:
                            dve.wait_ge(s_pe, c - 1)
                        nc.vector.tensor_copy(cnt_b[:, c % 2, :].rearrange("p (w o) -> p w o", o=HID),
                                              cnt[:, c, :].unsqueeze(2).to_broadcast([P, WMAX, HID]))
                        nc.vector.tensor_scalar(onehot[:, c % 2, 0:NGMAX - 1 + GROUPS], iota_g[:, :],
                                                g0[:, c:c + 1], None, ALU.is_equal).then_inc(s_dve, 1)
                    nc.vector.drain()
                    nc.vector.tensor_tensor(g0[:, :], g0[:, :], ngt[:, :], ALU.add)
                    nc.vector.tensor_tensor(loc_t, loc_t, ngt4[:, :].unsqueeze(2).to_broadcast([P, TROWS, P]),
                                            ALU.subtract)
                    dve.wait_ge(s_pe, TROWS)
                    for b, (g_at, g_n) in enumerate(GBANKS):
                        nc.vector.tensor_tensor(recip[:, g_at:g_at + g_n], recip[:, g_at:g_at + g_n],
                                                ps[:, b, 0:g_n], ALU.add)

                @block.tensor
                def _(pe):
                    for c in range(TROWS):
                        pe.wait_ge(s_dve, c + 1)
                        terms = [(g, cnt_b[:, c % 2, g * P:(g + 1) * P]) for g in range(NGMAX)]
                        group_products(terms, c).then_inc(s_pe, 1)
            stage_end()
        with nc.Block() as block:
            @block.vector
            def _(dve):
                nc.vector.tensor_scalar(recip[:, :], recip[:, :], 1.0, None, ALU.max)
                nc.vector.drain()
                nc.vector.reciprocal(recip[:, :], recip[:, :])
        stage_end()

        with nc.Fori(0, LAYERS) as layer:
            h_r = work[:, 0:16 * P].rearrange("p (q w) -> p q w", q=4)
            tab = mk_flat[:, 0:ROWS * JN * ROW_W]
            tab_b = tab.bitcast(BF16).rearrange("p (c j s h) -> p c j s h", c=ROWS, j=JN, s=PARTS)
            quads = [(q * 4, min(4, ROWS - q * 4)) for q in range(-(-ROWS // 4))]
            with nc.Block() as block:
                @block.sync
                def _(sp):
                    sp.dma_start(w2[:, :, :].rearrange("p k o -> p (k o)"),
                                 w2_b[bass.ds(layer, 1)].rearrange("a p w -> (a p) w")).then_inc(s_w, 16)
                    sp.dma_start(w1[:, :], w1_b[bass.ds(layer, 1)].rearrange("a p w -> (a p) w")).then_inc(s_w, 16)
                    sp.dma_start(rootw[:, :],
                                 root_b[bass.ds(layer, 1)].rearrange("a p w -> (a p) w")).then_inc(s_w, 16)
                    sp.dma_start(rootbias[:, :],
                                 root_bias[bass.ds(layer, 1)].rearrange("a p w -> (a p) w")).then_inc(s_w, 16)
                    sp.dma_start(local[:, :], local_dram).then_inc(s_w, 16)
                    sp.wait_ge(s_dve, 2 * len(quads) + 1)
                    sp.dma_start(table_rows, tab.bitcast(U32).rearrange("p (c w) -> p c w", c=ROWS)).then_inc(s_store, 16)
                    sp.wait_ge(s_store, 16)
                    sp.wait_ge(s_w, 80)

                @block.tensor
                def _(pe):
                    for c in range(ROWS):
                        last = nc.tensor.transpose(ps[:, c // 4, (c % 4) * P:(c % 4 + 1) * P],
                                                   node_h[:, c * P:(c + 1) * P], ident[:, :])
                        if c % 4 == 3 or c == ROWS - 1:
                            last.then_inc(s_pe, 1)

                @block.scalar
                def _(act):
                    for q, (c0, cn) in enumerate(quads):
                        src = ps[:, q, 0:cn * P].rearrange("p (c j h) -> p c j h", c=cn, j=JN)
                        act.wait_ge(s_pe, q + 1)
                        nc.scalar.copy(tab_b[:, c0:c0 + cn, :, 0, :], src).then_inc(s_act, 1)
                        act.wait_ge(s_dve, 2 * q + 2)
                        rest = h_r[:, q, 0:cn * P].rearrange("p (c j h) -> p c j h", c=cn, j=JN)
                        nc.scalar.copy(tab_b[:, c0:c0 + cn, :, 1, :], rest).then_inc(s_act, 1)

                @block.vector
                def _(dve):
                    nc.vector.memset(agg[:, :], 0.0)
                    nc.vector.tensor_copy(g0[:, :], g0_first[:, :]).then_inc(s_dve, 1)
                    for q, (c0, cn) in enumerate(quads):
                        src = ps[:, q, 0:cn * P].rearrange("p (c j h) -> p c j h", c=cn, j=JN)
                        rest = h_r[:, q, 0:cn * P].rearrange("p (c j h) -> p c j h", c=cn, j=JN)
                        dve.wait_ge(s_act, 2 * q + 1)
                        nc.vector.tensor_tensor(rest, src, tab_b[:, c0:c0 + cn, :, 0, :],
                                                ALU.subtract).then_inc(s_dve, 1)
                        dve.wait_ge(s_act, 2 * q + 2)
                        nc.vector.tensor_tensor(tab_b[:, c0:c0 + cn, :, 2, :], rest,
                                                tab_b[:, c0:c0 + cn, :, 1, :], ALU.subtract).then_inc(s_dve, 1)
            stage_end()

            with nc.Fori(0, n_passes) as _p:
                with nc.Block() as block:
                    @block.sync
                    def _(sp):
                        for n in range(2):
                            sp.dma_start(ea[0:SUB * EDGE_F, n, :, :].rearrange("p a e -> p (a e)"),
                                         ea_t[n]).then_inc(ea_in[n], 16)
                        with sp.Fori(0, CHUNKS) as i:
                            for s in range(SEGS):
                                sp.wait_ge(xm_done, i * (SEGS * SUBS) + (s * SUBS + 3))
                                sp.dma_start(idx[:, s, :],
                                             src_t[bass.ds(i * SEGS + s, 1)].rearrange("a p t -> (a p) t")
                                             ).then_inc(idx_in[s], 16)
                                sp.wait_ge(he_mm, i * SEGS + (s + 1))
                                sp.dma_start(ea[0:SUB * EDGE_F, (s + 2) % RING, :, :].rearrange("p a e -> p (a e)"),
                                             ea_t[bass.ds(i * SEGS + (s + 2), 1)].rearrange("a p w -> (a p) w")
                                             ).then_inc(ea_in[(s + 2) % RING], 16)

                    @block.gpsimd
                    def _(pool):
                        with pool.Fori(0, CHUNKS) as i:
                            for s in range(SEGS):
                                pool.wait_ge(idx_in[s], i * 16 + 16)
                                for q in range(SUBS):
                                    pool.wait_ge(xm_done, i * (SEGS * SUBS) + (s * SUBS + q + 1))
                                    nc.gpsimd.sem_inc(slot_taken, 1)
                                    for t in range(SUB):
                                        nc.gpsimd.indirect_dma_start(
                                            out=xg[:, s * SUBS + q, t, :], out_offset=None, in_=table,
                                            in_offset=bass.IndirectOffsetOnAxis(
                                                ap=idx[:, s, q * SUB + t:q * SUB + t + 1], axis=0),
                                        ).then_inc(gathered[s * SUBS + q], 16)
                        for n in range(GRING):
                            pool.wait_ge(gathered[n], CHUNKS * SUB * 16)

                    def he_rest(slot):
                        nc.vector.tensor_tensor(he_r[:, :, :], he32[:, slot, :, :], hp[:, slot, 0, :, 0:HID],
                                                ALU.subtract).then_inc(he_r1, 1)

                    def he_middle(slot):
                        nc.vector.tensor_copy(hp[:, slot, 1, :, 0:HID], he_r[:, :, :]).then_inc(he_mid, 1)

                    def he_low(slot):
                        nc.vector.tensor_tensor(hp[:, slot, 2, :, 0:HID], he_r[:, :, :],
                                                hp[:, slot, 1, :, 0:HID], ALU.subtract).then_inc(he_split, 1)

                    @block.vector
                    def _(dve):
                        nc.vector.sem_inc(xm_done, SEGS * SUBS)
                        dve.wait_ge(he_act, 1)
                        he_rest(0)
                        dve.wait_ge(he_r1, 1)
                        he_middle(0)
                        dve.wait_ge(he_mid, 1)
                        he_low(0)
                        for first, end, ng in WINDOWS:
                            w = JN * ng
                            with dve.Fori(first, end) as i:
                                for s in range(SEGS):
                                    nc.vector.tensor_tensor(
                                        eq[:, :, 0:w],
                                        local[:, bass.ds(i * CHUNK + s * SEG, SEG)].unsqueeze(2).to_broadcast([P, SEG, w]),
                                        iota_w[:, 0:w].unsqueeze(1).to_broadcast([P, SEG, w]),
                                        ALU.is_equal).then_inc(mask_eq, 1)
                                    dve.wait_ge(mask_eq, i * SEGS + (s + 1))
                                    nc.vector.tensor_scalar(mask[:, s, :, 0:w], eq[:, :, 0:w], -1, None,
                                                            ALU.mult).then_inc(mask_set, 1)
                                    dve.wait_ge(mask_set, i * SEGS + (s + 1))
                                    for q in range(SUBS):
                                        dve.wait_ge(gathered[s * SUBS + q], i * (SUB * 16) + SUB * 16)
                                        dve.wait_ge(units_done, i * (SEGS * SUBS) + (s * SUBS + q + 1))
                                        for a in range(PARTS):
                                            last = nc.vector.tensor_tensor(
                                                xm[:, q, a * SUB * w * PW:(a + 1) * SUB * w * PW].rearrange(
                                                    "p (t w c) -> p t w c", t=SUB, w=w),
                                                xg[:, s * SUBS + q, :, a * PW:(a + 1) * PW].unsqueeze(2).to_broadcast([P, SUB, w, PW]),
                                                mask[:, s, q * SUB:(q + 1) * SUB, 0:w].bitcast(U32).unsqueeze(3).to_broadcast(
                                                    [P, SUB, w, PW]),
                                                ALU.bitwise_and)
                                        last.then_inc(xm_done, 1)
                                        if q == 0:
                                            dve.wait_ge(he_act, i * SEGS + (s + 2))
                                            he_rest((s + 1) % RING)
                                        elif q == 1:
                                            dve.wait_ge(he_r1, i * SEGS + (s + 2))
                                            he_middle((s + 1) % RING)
                                        else:
                                            dve.wait_ge(he_mid, i * SEGS + (s + 2))
                                            he_low((s + 1) % RING)
                        nc.vector.drain()
                        nc.vector.tensor_tensor(g0_next[:, :], g0[:, :], ngt[:, :], ALU.add)
                        for first, end, ng in WINDOWS:
                            nc.vector.tensor_scalar(local[:, first * CHUNK:end * CHUNK],
                                                    local[:, first * CHUNK:end * CHUNK],
                                                    float(-JN * ng), None, ALU.add)

                    def he_products(slot):
                        for a in range(SUBS):
                            last = nc.tensor.matmul(he_ps[:, a, 0:SUB * HID], ea[:, slot, a, :], w1[:, :],
                                                    start=True, stop=True)
                        last.then_inc(he_mm, 1)

                    @block.tensor
                    def _(pe):
                        nc.tensor.sem_inc(units_done, SUBS)
                        nc.tensor.sem_inc(he_mm, 1)
                        for n in range(2):
                            pe.wait_ge(ea_in[n], 16)
                            if n:
                                pe.wait_ge(he_act, n)
                            he_products(n)
                        for first, end, ng in WINDOWS:
                            with pe.Fori(first, end) as i:
                                for s in range(SEGS):
                                    pe.wait_ge(ea_in[(s + 2) % RING], i * 16 + (16 if s == 0 else 32))
                                    pe.wait_ge(he_act, i * SEGS + (s + 2))
                                    if s == 0:
                                        pe.wait_ge(r_done, i + 1)
                                    he_products((s + 2) % RING)
                                    pe.wait_ge(he_split, i * SEGS + (s + 1))
                                    for q in range(SUBS):
                                        pe.wait_ge(xm_done, i * (SEGS * SUBS) + (s * SUBS + q + 10))
                                        pe.wait_ge(evac, i * (SEGS * SUBS) + (s * SUBS + q + 1))
                                        xb = xm[:, q, 0:PARTS * SUB * JN * ng * PW].bitcast(BF16).rearrange(
                                            "p (a u c) -> p a u c", a=PARTS, u=SUB * ng)
                                        for t in range(SUB):
                                            for g in range(ng):
                                                u = (t % 3) * ng + g
                                                for n, (a, b) in enumerate(PRODUCTS):
                                                    last = nc.tensor.matmul(
                                                        ps[:, 2 * q + t // 3, u * K1:(u + 1) * K1],
                                                        xb[:, a, t * ng + g, :], hp[:, s, b, q * SUB + t, :],
                                                        start=n == 0, stop=n == len(PRODUCTS) - 1)
                                        last.then_inc(units_done, 1)
                                pe.wait_ge(evac, i * (SEGS * SUBS) + (SEGS * SUBS + SUBS))
                                pe.wait_ge(he_act, i * SEGS + (SEGS + 2))
                                for k in range(K1):
                                    last = nc.tensor.matmul(contr[:, 0:CHUNK * ng], w2[:, k, :],
                                                            mk[:, k, 0:CHUNK * ng], start=k == 0, stop=k == K1 - 1)
                                last.then_inc(contr_done, 1)

                    def he_high(slot):
                        he = he_ps[:, :, 0:SUB * HID]
                        nc.scalar.activation(he32[:, slot, :, :].rearrange("p (a t) h -> p a (t h)", a=SUBS), he, ACT.Relu)
                        for a in range(SUBS):
                            last = nc.scalar.activation(hp[:, slot, 0, a * SUB:(a + 1) * SUB, 0:HID],
                                                        he_ps[:, a, 0:SUB * HID].rearrange("p (t h) -> p t h", h=HID),
                                                        ACT.Relu)
                        last.then_inc(he_act, 1)

                    @block.scalar
                    def _(act):
                        nc.scalar.sem_inc(evac, SUBS)
                        nc.scalar.sem_inc(r_done, 1)
                        for n in range(2):
                            act.wait_ge(he_mm, n + 2)
                            he_high(n)
                        for first, end, ng in WINDOWS:
                            with act.Fori(first, end) as i:
                                for s in range(SEGS):
                                    for q in range(SUBS):
                                        n = s * SUBS + q
                                        if q == 0:
                                            act.wait_ge(he_mm, i * SEGS + (s + 4))
                                            act.wait_ge(units_done, i * (SEGS * SUBS) + (s * SUBS + 3))
                                            he_high((s + 2) % RING)
                                        act.wait_ge(units_done, i * (SEGS * SUBS) + (n + 4))
                                        nc.scalar.copy(
                                            mk[:, :, n * SUB * ng:(n + 1) * SUB * ng].rearrange(
                                                "p k (b u) -> p b u k", b=2),
                                            ps[:, 2 * q:2 * q + 2, 0:3 * ng * K1].rearrange(
                                                "p b (u k) -> p b u k", k=K1)).then_inc(evac, 1)
                                act.wait_ge(contr_done, i + 1)
                                nc.scalar.copy(msg_t[:, 0:ng, bass.ds(i * CHUNK, CHUNK)],
                                               contr[:, 0:CHUNK * ng].rearrange("p (t g) -> p g t", g=ng)
                                               ).then_inc(r_done, 1)
                stage_end()

                with nc.Block() as block:
                    @block.tensor
                    def _(pe):
                        def to_rows(c):
                            if c >= 2:
                                pe.wait_ge(s_dve, c - 1)
                            for g in range(NGMAX):
                                last = nc.tensor.transpose(ps[:, 4 + c % 2, g * P:(g + 1) * P],
                                                           msg_t[:, g, c * P:(c + 1) * P], ident[:, :])
                            last.then_inc(s_pe, 1)

                        to_rows(0)
                        for c in range(TROWS):
                            if c + 1 < TROWS:
                                to_rows(c + 1)
                            pe.wait_ge(s_dve, c + 1)
                            terms = [(g, r_parts[:, c % 2, a, g * P:(g + 1) * P])
                                     for g in range(NGMAX) for a in range(PARTS)]
                            group_products(terms, c).then_inc(s_pool, 1)

                    @block.scalar
                    def _(act):
                        for c in range(TROWS):
                            act.wait_ge(s_pe, c + 1)
                            if c >= 2:
                                act.wait_ge(s_pool, c - 1)
                            nc.scalar.copy(r_parts[:, c % 2, 0, :], ps[:, 4 + c % 2, :]).then_inc(s_act, 1)
                            act.wait_ge(s_load, c + 1)
                            nc.scalar.copy(r_parts[:, c % 2, 1, :], r_rest[:, c % 2, :]).then_inc(s_act, 1)

                    @block.vector
                    def _(dve):
                        for c in range(TROWS):
                            if c >= 2:
                                dve.wait_ge(s_pool, c - 1)
                            nc.vector.tensor_scalar(onehot[:, c % 2, 0:NGMAX - 1 + GROUPS], iota_g[:, :],
                                                    g0[:, c:c + 1], None, ALU.is_equal)
                            dve.wait_ge(s_act, 2 * c + 1)
                            nc.vector.tensor_tensor(r_rest[:, c % 2, :], ps[:, 4 + c % 2, :],
                                                    r_parts[:, c % 2, 0, :], ALU.subtract).then_inc(s_load, 1)
                            dve.wait_ge(s_act, 2 * c + 2)
                            nc.vector.tensor_tensor(r_parts[:, c % 2, 2, :], r_rest[:, c % 2, :],
                                                    r_parts[:, c % 2, 1, :], ALU.subtract).then_inc(s_dve, 1)
                        nc.vector.drain()
                        nc.vector.tensor_copy(g0[:, :], g0_next[:, :])
                        dve.wait_ge(s_pool, TROWS)
                        for b, (g_at, g_n) in enumerate(GBANKS):
                            nc.vector.tensor_tensor(agg[:, g_at:g_at + g_n], agg[:, g_at:g_at + g_n],
                                                    ps[:, b, 0:g_n], ALU.add)
                stage_end()

            with nc.Block() as block:
                @block.tensor
                def _(pe):
                    for b, (g_at, g_n) in enumerate(GBANKS):
                        nc.tensor.matmul(ps[:, b, 0:g_n], rootw[:, :], node_h[:, g_at:g_at + g_n],
                                         start=True, stop=True).then_inc(s_pe, 1)

                @block.vector
                def _(dve):
                    nc.vector.tensor_tensor(agg[:, :], agg[:, :], recip[:, :], ALU.mult)
                    nc.vector.drain()
                    for b, (g_at, g_n) in enumerate(GBANKS):
                        dve.wait_ge(s_pe, b + 1)
                        nc.vector.tensor_tensor(agg[:, g_at:g_at + g_n], agg[:, g_at:g_at + g_n],
                                                ps[:, b, 0:g_n], ALU.add).then_inc(s_dve, 1)

                @block.scalar
                def _(act):
                    for b, (g_at, g_n) in enumerate(GBANKS):
                        act.wait_ge(s_dve, b + 1)
                        act.wait_ge(s_pe, b + 1)
                        nc.scalar.activation(node_h[:, g_at:g_at + g_n], agg[:, g_at:g_at + g_n], ACT.Relu,
                                             bias=rootbias[:, 0:1])
            stage_end()

        z_t = work[:, 0:GPAD]
        d_t = work[:, GPAD:2 * GPAD]
        x_res = work[:, 2 * GPAD:2 * GPAD + XW].rearrange("p (c w) -> p c w", c=ROWS)
        y = mk_flat[:, 0:XW].rearrange("p (c w) -> p c w", c=ROWS)
        wout = mk_flat[:, XW:XW + JN * LAT]
        wdec1 = mk_flat[:, XW + 64:XW + 64 + P]
        wdec2 = mk_flat[:, XW + 192:XW + 192 + JN * NODE_F]
        bdec2 = mk_flat[:, XW + 448:XW + 448 + JN * NODE_F]
        FW = GPAD // 4
        with nc.Block() as block:
            @block.sync
            def _(sp):
                sp.dma_start(wout, lout_b).then_inc(s_w, 16)
                sp.dma_start(biases[0:JN * LAT, 1:2], lout_bias).then_inc(s_w, 16)
                sp.dma_start(wdec1[0:JN * LAT, :], dec1_b).then_inc(s_w, 16)
                sp.dma_start(biases[:, 2:3], dec1_bias).then_inc(s_w, 16)
                sp.dma_start(wdec2, dec2_b).then_inc(s_w, 16)
                sp.dma_start(bdec2, dec2_bias).then_inc(s_w, 16)
                sp.dma_start(x_res, x_rows).then_inc(s_load, 16)
                sp.wait_ge(s_dve, ROWS + 1)
                sp.dma_start(out, y).then_inc(s_store, 16)
                sp.wait_ge(s_store, 16)

            @block.tensor
            def _(pe):
                pe.wait_ge(s_w, 96)
                for b in range(4):
                    nc.tensor.matmul(ps[0:JN * LAT, b, 0:FW], wout, node_h[:, b * FW:(b + 1) * FW],
                                     start=True, stop=True).then_inc(s_pe, 1)
                for b in range(4):
                    pe.wait_ge(s_act, b + 1)
                    nc.tensor.matmul(ps[:, 4 + b, 0:FW], wdec1[0:JN * LAT, :],
                                     z_t[0:JN * LAT, b * FW:(b + 1) * FW],
                                     start=True, stop=True).then_inc(s_pe, 1)
                pe.wait_ge(s_act, 8)
                for c in range(ROWS):
                    if c >= 4:
                        pe.wait_ge(s_dve, 1 + c - 3)
                    nc.tensor.matmul(ps[:, c % 4, 0:JN * NODE_F], d_t[:, c * P:(c + 1) * P], wdec2,
                                     start=True, stop=True).then_inc(s_pe, 1)

            @block.scalar
            def _(act):
                act.wait_ge(s_w, 96)
                for b in range(4):
                    act.wait_ge(s_pe, b + 1)
                    nc.scalar.activation(z_t[0:JN * LAT, b * FW:(b + 1) * FW], ps[0:JN * LAT, b, 0:FW],
                                         ACT.Identity, bias=biases[0:JN * LAT, 1:2]).then_inc(s_act, 1)
                for b in range(4):
                    act.wait_ge(s_pe, 4 + b + 1)
                    nc.scalar.activation(d_t[:, b * FW:(b + 1) * FW], ps[:, 4 + b, 0:FW], ACT.Relu,
                                         bias=biases[:, 2:3]).then_inc(s_act, 1)

            @block.vector
            def _(dve):
                dve.wait_ge(s_w, 96)
                dve.wait_ge(s_load, 16)
                nc.vector.tensor_tensor(x_res, x_res, bdec2.unsqueeze(1).to_broadcast([P, ROWS, JN * NODE_F]),
                                        ALU.add).then_inc(s_dve, 1)
                dve.wait_ge(s_dve, 1)
                for c in range(ROWS):
                    dve.wait_ge(s_pe, 8 + c + 1)
                    nc.vector.tensor_tensor(y[:, c, :], ps[:, c % 4, 0:JN * NODE_F], x_res[:, c, :],
                                            ALU.add).then_inc(s_dve, 1)


def kernel(**inputs):
    import numpy as np

    import concourse.bacc as bacc
    from concourse.bass_utils import run_bass_kernel_spmd

    a = {k.replace("L0_gnn_", ""): np.asarray(v) for k, v in inputs.items()}

    def diagonal(w, n):
        *lead, r, c = w.shape
        m = np.zeros((*lead, n * r, n * c), w.dtype)
        for j in range(n):
            m[..., j * r:(j + 1) * r, j * c:(j + 1) * c] = w
        return m

    def padded(x, n, fill=0):
        return np.concatenate([x, np.full((n - x.shape[0], *x.shape[1:]), fill, x.dtype)])

    def by_row(x):
        return np.ascontiguousarray(x)

    x = padded(a["x"], GPAD * JN)
    x_rows = by_row(x.reshape(ROWS, P, JN * NODE_F).transpose(1, 0, 2))
    n_e = TILES * P
    src_t = by_row(padded(a["src"], n_e).reshape(CHUNKS * SEGS, SEG, P).transpose(0, 2, 1))
    dst_t = by_row(padded(a["dst"], TPAD * P, -1).reshape(TROWS, P, P).transpose(1, 0, 2).reshape(P, TPAD))
    ea = padded(a["edge_attr_16"], HE_SEGS * SEG * P).reshape(HE_SEGS, SUBS, SUB, P, EDGE_F)
    ea_t = by_row(ea.transpose(0, 2, 4, 1, 3).reshape(HE_SEGS, SUB * EDGE_F, SUBS * P))

    w1_b = np.concatenate([diagonal(a["edge_w1"], SUB), np.tile(a["edge_b1"], SUB)[:, None, :]], 1)
    w2 = np.concatenate([a["edge_w2"], a["edge_b2"][:, None, :]], 1).reshape(LAYERS, K1, HID, HID)
    w2_b = by_row(diagonal(w2, JN).transpose(0, 2, 1, 3).reshape(LAYERS, P, K1 * P))
    root_b = diagonal(a["root_w"], JN)
    root_bias = np.tile(a["root_b"], JN)[:, :, None]
    lin_w = np.zeros((P, 2, P), a["lin_in_w"].dtype)
    for h in range(2):
        lin_w[:, h, h * 2 * HID:(h + 1) * 2 * HID] = diagonal(a["lin_in_w"], 2)

    tile_groups = np.array([groups_of_tile(t) for t in range(TPAD)], np.float32).reshape(TROWS, P).T
    window = np.arange(WMAX)[None, None, :] < JN * tile_groups[:, :, None]
    arrays = {
        "x_rows": x_rows, "src_t": src_t, "dst_t": dst_t, "ea_t": ea_t, "w1_b": w1_b, "w2_b": w2_b,
        "root_b": root_b, "root_bias": root_bias, "lin_w": lin_w,
        "lin_bias": np.tile(a["lin_in_b"], JN)[:, None],
        "lout_b": diagonal(a["lin_out_w"], JN), "lout_bias": np.tile(a["lin_out_b"], JN)[:, None],
        "dec1_b": diagonal(a["dec_w1"], JN), "dec1_bias": np.tile(a["dec_b1"], JN)[:, None],
        "dec2_b": diagonal(a["dec_w2"], JN), "dec2_bias": np.tile(a["dec_b2"], (P, JN)),
        "tile_ng": tile_groups, "tile_valid": window.reshape(P, TROWS * WMAX).astype(np.float32),
        "tile_scale": LCM / tile_groups,
    }
    arrays = {k: np.ascontiguousarray(v) for k, v in arrays.items()}
    nc = bacc.Bacc("TRN2", target_bir_lowering=False, num_devices=1)
    aps = {k: nc.dram_tensor(k, v.shape, mybir.dt.from_np(v.dtype), kind="ExternalInput").ap()
           for k, v in arrays.items()}
    aps["src_t"] = aps["src_t"].bitcast(U32)
    out = nc.dram_tensor("out_rows", (P, ROWS, JN * NODE_F), F32, kind="ExternalOutput").ap()
    gnn_program(nc, **aps, out=out)
    r = run_bass_kernel_spmd(nc, [arrays], core_ids=[0])
    rows = np.asarray(r.results[0]["out_rows"])
    return rows.transpose(1, 0, 2).reshape(GPAD * JN, NODE_F)[:N_NODES]
```

```python
from contextlib import ExitStack

import concourse.bass as bass
from concourse import mybir

F32 = mybir.dt.float32
BF16 = mybir.dt.bfloat16
I32 = mybir.dt.int32
U32 = mybir.dt.uint32
ALU = mybir.AluOpType
ACT = mybir.ActivationFunctionType
AX = mybir.AxisListType

P = 128
N_NODES = 6250
N_EDGES = 200000
NODE_F = 64
EDGE_F = 16
HID = 32
LAT = 16
LAYERS = 3
EPS = 1e-5

JN = P // HID
GROUPS = -(-N_NODES // JN)
ROWS = -(-GROUPS // P)
GPAD = ROWS * P
HALF = ROWS // 2
GBANK = -(-GROUPS // 4)
GBANKS = [(b * GBANK, min(GBANK, GROUPS - b * GBANK)) for b in range(4)]
BAND = 256
BANDS = -(-GROUPS // BAND)

SUB = 6
SUBS = 3
SEG = SUB * SUBS
SEGS = 3
CHUNK = SEG * SEGS
CHUNKS = -(-N_EDGES // (P * CHUNK))
TILES = CHUNKS * CHUNK
TROWS = -(-TILES // P)
TPAD = TROWS * P
RING = 3
GRING = SEGS * SUBS
HE_SEGS = CHUNKS * SEGS + 2

WINDOWS = [(0, 11, 4), (11, 20, 3), (20, CHUNKS, 2)]
NGMAX = 4
WMAX = JN * NGMAX
K1 = HID + 1
PARTS = 3
PW = HID // 2
ROW_W = PARTS * PW
FAR = 1 << 20
LCM = 12


PRODUCTS = [(0, 2), (0, 1), (0, 0), (1, 1), (1, 0), (2, 0)]


def groups_of_tile(t):
    c = min(t // CHUNK, CHUNKS - 1)
    return next(ng for a, b, ng in WINDOWS if a <= c < b)


def groups_of_block(c):
    return max(groups_of_tile(t) for t in range(c * P, min((c + 1) * P, TILES)))


def blocks_with(w):
    return sum(w < JN * groups_of_block(c) for c in range(TROWS))


def gnn_program(nc, x_rows, src_t, dst_t, ea_t, w1_b, w2_b, root_b, root_bias, lin_w, lin_bias,
                lout_b, lout_bias, dec1_b, dec1_bias, dec2_b, dec2_bias, tile_ng, tile_valid,
                tile_scale, out):
    table = nc.dram_tensor("node_table", (GPAD * JN, ROW_W), U32, kind="Internal").ap()
    local_dram = nc.dram_tensor("local_of_edge", (P, TPAD), F32, kind="Internal").ap()
    table_rows = table.rearrange("(c p j) w -> p c (j w)", p=P, j=JN)

    with ExitStack() as ctx:
        def sb(name, shape, dt=F32):
            return ctx.enter_context(nc.sbuf_tensor(name, shape, dt))

        sem_list = []

        def sem(name):
            s = ctx.enter_context(nc.semaphore(name))
            sem_list.append(s)
            return s

        ps = ctx.enter_context(nc.psum_tensor("ps", [P, 8, 512], F32))

        ident = sb("ident", [P, P])
        node_h = sb("node_h", [P, GPAD])
        agg = sb("agg", [P, GROUPS - 1 + BANDS * BAND])
        recip = sb("recip", [P, GROUPS])
        iota_g = sb("iota_g", [P, NGMAX - 1 + BAND])
        iota_w = sb("iota_w", [P, WMAX])
        local = sb("local", [P, TPAD])
        g0_first = sb("g0_first", [P, TROWS])
        g0 = sb("g0", [P, TROWS])
        ngt = sb("ngt", [P, TROWS])
        g0_band = sb("g0_band", [P, TROWS])
        counts_i = sb("counts_i", [P, 2 * TROWS + 2], I32)
        msg_t = sb("msg_t", [P, NGMAX, TPAD])
        onehot = sb("onehot", [P, RING, NGMAX + BAND], BF16)
        w2 = sb("w2", [P, K1, P])
        w1 = sb("w1", [SUB * EDGE_F + 1, SUB * HID])
        rootw = sb("rootw", [P, P])
        rootbias = sb("rootbias", [P, 1])
        ea = sb("ea", [SUB * EDGE_F + 1, RING, SUBS, P])
        idx = sb("idx", [P, RING, SEG], U32)
        xg = sb("xg", [P, GRING, SUB, ROW_W], U32)
        eq = sb("eq", [P, SEG, WMAX], I32)
        mask = sb("mask", [P, RING, SEG, WMAX], I32)
        he32 = sb("he32", [P, RING, SEG, HID])
        he_r = sb("he_r", [P, SEG, HID])
        hp = sb("hp", [P, RING, PARTS, SEG, K1], BF16)

        XM_W = PARTS * SUB * WMAX * PW
        work = sb("work", [P, RING * XM_W])
        xm = work[:, :].bitcast(U32).rearrange("p (s w) -> p s w", s=RING)
        mk = sb("mk", [P, K1, CHUNK * NGMAX])
        mk_flat = mk[:, :, :].rearrange("p k u -> p (k u)")

        XW = ROWS * JN * NODE_F
        x_in = work[:, 0:XW]
        x_c = work[:, XW:2 * XW]
        x_s = work[:, 2 * XW:3 * XW]
        x_t = work[:, 3 * XW:4 * XW].rearrange("p (a g) -> p a g", a=2)
        LT_W = TROWS * P
        loc_t = mk_flat[:, 0:LT_W].rearrange("p (c e) -> p c e", c=TROWS)
        dst_i = mk_flat[:, LT_W:2 * LT_W].bitcast(I32)
        dst_f = mk_flat[:, 2 * LT_W:3 * LT_W]
        iota_i = mk_flat[:, 3 * LT_W:3 * LT_W + NGMAX - 1 + BAND].bitcast(I32)
        dst_m = node_h[:, :]
        local_b = mk_flat[:, 0:TPAD // 2].bitcast(BF16)
        into = work[:, 0:WMAX * TPAD // 2].bitcast(BF16).rearrange("p (w t) -> p w t", w=WMAX)
        cnt = mk_flat[:, 6000:6000 + TROWS * WMAX].rearrange("p (c w) -> p c w", c=TROWS)
        valid = mk_flat[:, 6256:6256 + TROWS * WMAX]
        cnt_b = mk_flat[:, 3200:3200 + RING * WMAX * HID // 2].bitcast(BF16).rearrange("p (d w) -> p d w", d=RING)
        he_ps = ps[:, 6:8, :].rearrange("p b c -> p (b c)").rearrange("p (a c) -> p a c", a=4)[:, 0:SUBS, :]
        contr = ps[:, 7, 256:512]
        r_parts = work[:, 0:RING * PARTS * 256].bitcast(BF16).rearrange("p (d a w) -> p d a w", d=RING, a=PARTS)
        r_rest = work[:, RING * PARTS * 256:RING * PARTS * 256 + RING * 512].rearrange("p (d w) -> p d w", d=RING)
        small = sb("small", [P, 8, ROWS * JN])
        ones = sb("ones", [P, 2], BF16)
        prew = sb("prew", [P, 2, P])
        biases = sb("biases", [P, 4])

        centred = sem("centred")
        squared = sem("squared")
        s_load = sem("s_load")
        s_w = sem("s_w")
        s_dve = sem("s_dve")
        s_act = sem("s_act")
        s_pe = sem("s_pe")
        s_pool = sem("s_pool")
        s_store = sem("s_store")
        idx_in = [sem(f"idx_in{i}") for i in range(RING)]
        ea_in = [sem(f"ea_in{i}") for i in range(RING)]
        gathered = [sem(f"gathered{i}") for i in range(GRING)]
        slot_taken = sem("slot_taken")
        mask_eq = sem("mask_eq")
        mask_set = sem("mask_set")
        xm_done = sem("xm_done")
        units_done = sem("units_done")
        he_mm = sem("he_mm")
        he_act = sem("he_act")
        he_r1 = sem("he_r1")
        he_mid = sem("he_mid")
        he_split = sem("he_split")
        evac = sem("evac")
        contr_done = sem("contr_done")
        r_done = sem("r_done")

        def stage_end():
            nums = [s.num for s in sem_list]
            assert max(nums) - min(nums) == len(nums) - 1
            nc.gpsimd.dma_reset(range(min(nums), max(nums) + 1))
            nc.gpsimd.sem_clear(range(min(nums), max(nums) + 1))
            nc.all_engine_barrier(sem_only=True)

        halves = [(0, HALF), (HALF, ROWS)]

        with nc.Block() as block:
            @block.sync
            def _(sp):
                sp.dma_start(dst_i, dst_t).then_inc(s_load, 16)
                sp.dma_start(ngt[:, :], tile_ng).then_inc(s_load, 16)
                sp.dma_start(idx[:, 0, :], src_t[0]).then_inc(s_load, 16)
                sp.dma_start(small[:, 7, 0:TROWS], tile_scale).then_inc(s_load, 16)
                sp.dma_start(valid, tile_valid).then_inc(s_load, 16)
                sp.dma_start(prew[:, :, :], lin_w).then_inc(s_w, 16)
                sp.dma_start(biases[:, 0:1], lin_bias).then_inc(s_w, 16)
                sp.dma_start(x_in.rearrange("p (c w) -> p c w", c=ROWS), x_rows).then_inc(s_w, 16)
                sp.wait_ge(s_act, TROWS)
                sp.dma_start(local_dram, local[:, :]).then_inc(s_store, 16)
                sp.wait_ge(s_store, 16)

            @block.gpsimd
            def _(pool):
                nc.gpsimd.memset(ident[:, :], 0.0).then_inc(s_pool, 1)
                nc.gpsimd.iota(iota_i, pattern=[[1, NGMAX - 1 + BAND]], base=-(NGMAX - 1),
                               channel_multiplier=0).then_inc(s_pool, 1)
                pool.wait_ge(s_pool, 2)
                nc.gpsimd.affine_select(out=ident[:, :], in_=ident[:, :], compare_op=ALU.not_equal, fill=1.0,
                                        base=0, pattern=[[-1, P]], channel_multiplier=1).then_inc(s_pool, 1)
                pool.wait_ge(s_pool, 3)
                nc.gpsimd.memset(msg_t[:, :, :], 0.0)
                nc.gpsimd.memset(agg[:, :], 0.0)
                nc.gpsimd.memset(hp[:, :, :, :, :], 0.0).then_inc(s_pool, 1)
                pool.wait_ge(s_pool, 4)
                nc.gpsimd.memset(hp[:, :, 0, :, HID:K1], 1.0).then_inc(s_pool, 1)
                pool.wait_ge(s_dve, 8)
                nc.gpsimd.partition_all_reduce(small[:, 7, 0:2 * TROWS + 1], small[:, 6, 0:2 * TROWS + 1], P,
                                               bass.bass_isa.ReduceOp.max).then_inc(s_pool, 1)

            @block.vector
            def _(dve):
                nc.vector.memset(ea[SUB * EDGE_F:SUB * EDGE_F + 1, :, :, :], 1.0)
                dve.wait_ge(s_load, 80)
                nc.vector.memset(ones[:, :], 1.0)
                nc.vector.tensor_copy(dst_f, dst_i).then_inc(s_dve, 1)
                dve.wait_ge(s_dve, 1)
                nc.vector.tensor_scalar(dst_m, dst_f, 0.0, float(FAR), ALU.is_lt, ALU.mult).then_inc(s_dve, 1)
                dve.wait_ge(s_dve, 2)
                nc.vector.tensor_tensor(dst_m, dst_m, dst_f, ALU.add).then_inc(s_dve, 1)
                dve.wait_ge(s_dve, 3)
                nc.vector.tensor_reduce(small[:, 0, 0:TROWS], dst_m.rearrange("p (c e) -> p c e", c=TROWS),
                                        axis=AX.X, op=ALU.min)
                nc.vector.tensor_reduce(small[:, 1, 0:TROWS], dst_f.rearrange("p (c e) -> p c e", c=TROWS),
                                        axis=AX.X, op=ALU.max).then_inc(s_dve, 1)
                dve.wait_ge(s_dve, 4)
                lo_i = small[:, 2, 0:TROWS].bitcast(I32)
                hi_i = small[:, 3, 0:TROWS].bitcast(I32)
                nc.vector.tensor_copy(lo_i, small[:, 0, 0:TROWS])
                nc.vector.tensor_copy(hi_i, small[:, 1, 0:TROWS]).then_inc(s_dve, 1)
                dve.wait_ge(s_dve, 5)
                lo_g = small[:, 4, 0:TROWS].bitcast(I32)
                hi_g = small[:, 5, 0:TROWS].bitcast(I32)
                nc.vector.tensor_scalar(lo_g, lo_i, 2, None, ALU.arith_shift_right)
                nc.vector.tensor_scalar(hi_g, hi_i, 2, None, ALU.arith_shift_right).then_inc(s_dve, 1)
                dve.wait_ge(s_dve, 6)
                nc.vector.tensor_copy(g0_first[:, :], lo_g)
                nc.vector.tensor_copy(small[:, 0, 0:TROWS], hi_g).then_inc(s_dve, 1)
                dve.wait_ge(s_dve, 7)
                nc.vector.tensor_tensor(small[:, 1, 0:TROWS], small[:, 0, 0:TROWS], g0_first[:, :], ALU.subtract)
                nc.vector.tensor_scalar(small[:, 2, 0:TROWS], g0_first[:, :], float(JN), None, ALU.mult)
                nc.vector.drain()
                nc.vector.scalar_tensor_tensor(small[:, 3, 0:TROWS], small[:, 1, 0:TROWS], 1.0,
                                               small[:, 7, 0:TROWS], ALU.add, ALU.mult)
                nc.vector.drain()
                nc.vector.tensor_scalar(small[:, 6, 0:TROWS], g0_first[:, :], -1.0, None, ALU.mult)
                nc.vector.tensor_copy(small[:, 6, TROWS:2 * TROWS], small[:, 0, 0:TROWS])
                nc.vector.tensor_reduce(small[:, 6, 2 * TROWS:2 * TROWS + 1], small[:, 3, 0:TROWS], axis=AX.X,
                                        op=ALU.max).then_inc(s_dve, 1)
                nc.vector.tensor_tensor(loc_t, dst_f.rearrange("p (c e) -> p c e", c=TROWS),
                                        small[:, 2, 0:TROWS].unsqueeze(2).to_broadcast([P, TROWS, P]),
                                        ALU.subtract).then_inc(s_dve, 1)
                dve.wait_ge(s_pool, 5)
                nc.vector.tensor_copy(iota_g[:, :], iota_i).then_inc(s_dve, 1)
                dve.wait_ge(s_dve, 10)
                nc.vector.tensor_scalar(iota_w[:, :], iota_g[:, NGMAX - 1:NGMAX - 1 + WMAX], 0.0, None, ALU.add)
                dve.wait_ge(s_pool, 6)
                first, last = small[:, 7, 0:TROWS], small[:, 7, TROWS:2 * TROWS]
                nc.vector.tensor_tensor(g0[:, :], g0_first[:, :], first, ALU.add)
                nc.vector.tensor_tensor(last, last, first, ALU.add)
                nc.vector.drain()
                nc.vector.tensor_copy(g0_first[:, :], g0[:, :])
                nc.vector.tensor_scalar(counts_i[:, 0:TROWS], first, -1.0, None, ALU.mult)
                nc.vector.tensor_copy(counts_i[:, TROWS:2 * TROWS + 1], small[:, 7, TROWS:2 * TROWS + 1])
                nc.vector.drain()
                nc.vector.tensor_scalar(small[:, 5, 0:TROWS].bitcast(I32), counts_i[:, TROWS:2 * TROWS],
                                        BAND.bit_length() - 1, None, ALU.arith_shift_right)
                nc.vector.drain()
                nc.vector.tensor_copy(small[:, 6, 0:TROWS], small[:, 5, 0:TROWS].bitcast(I32))
                nc.vector.drain()
                nc.vector.tensor_reduce(small[:, 6, TROWS:TROWS + 1], small[:, 6, 0:TROWS], axis=AX.X, op=ALU.max)
                nc.vector.drain()
                nc.vector.tensor_scalar(counts_i[:, 2 * TROWS + 1:2 * TROWS + 2], small[:, 6, TROWS:TROWS + 1],
                                        1.0, None, ALU.add).then_inc(s_dve, 1)

                dve.wait_ge(s_w, 48)
                x3 = x_in.rearrange("p (n f) -> p n f", f=NODE_F)
                c3 = x_c.rearrange("p (n f) -> p n f", f=NODE_F)
                s3 = x_s.rearrange("p (n f) -> p n f", f=NODE_F)
                nc.vector.tensor_reduce(small[:, 0, :], x3, axis=AX.X, op=ALU.add)
                nc.vector.drain()
                nc.vector.tensor_scalar(small[:, 1, :], small[:, 0, :], 1.0 / NODE_F, None, ALU.mult)
                nc.vector.drain()
                for c0, c1 in halves:
                    rows = slice(c0 * JN, c1 * JN)
                    nc.vector.tensor_tensor(c3[:, rows, :], x3[:, rows, :], small[:, 1, rows].unsqueeze(2).to_broadcast(
                        [P, (c1 - c0) * JN, NODE_F]), ALU.subtract).then_inc(centred, 1)
                for half, (c0, c1) in enumerate(halves):
                    rows = slice(c0 * JN, c1 * JN)
                    dve.wait_ge(squared, half + 1)
                    nc.vector.tensor_reduce(small[:, 2, rows], s3[:, rows, :], axis=AX.X, op=ALU.add)
                nc.vector.drain()
                nc.vector.tensor_scalar(small[:, 3, :], small[:, 2, :], 1.0 / NODE_F, EPS, ALU.mult,
                                        ALU.add).then_inc(s_dve, 1)
                dve.wait_ge(s_act, TROWS + 1)
                nc.vector.reciprocal(small[:, 5, :], small[:, 4, :])
                nc.vector.drain()
                for c0, c1 in halves:
                    rows = slice(c0 * JN, c1 * JN)
                    nc.vector.tensor_tensor(s3[:, rows, :], c3[:, rows, :], small[:, 5, rows].unsqueeze(2).to_broadcast(
                        [P, (c1 - c0) * JN, NODE_F]), ALU.mult).then_inc(s_dve, 1)

            @block.tensor
            def _(pe):
                pe.wait_ge(s_dve, 9)
                pe.wait_ge(s_pool, 3)
                for c in range(TROWS):
                    if c >= 4:
                        pe.wait_ge(s_act, c - 3)
                    nc.tensor.transpose(ps[:, c % 4, 0:P], loc_t[:, c, :], ident[:, :]).then_inc(s_pe, 1)
                for n in range(2 * ROWS):
                    pe.wait_ge(s_dve, 13 if n < 2 * HALF else 14)
                    if n >= 4:
                        pe.wait_ge(s_act, TROWS + 1 + n - 3)
                    nc.tensor.transpose(ps[:, 4 + n % 4, 0:P], x_s[:, n * P:(n + 1) * P],
                                        ident[:, :]).then_inc(s_pe, 1)
                pe.wait_ge(s_act, TROWS + 1 + 2 * ROWS)
                pe.wait_ge(s_w, 48)
                for b in range(4):
                    w = GPAD // 4
                    for a in range(2):
                        last = nc.tensor.matmul(ps[:, b, 0:w], prew[:, a, :], x_t[:, a, b * w:(b + 1) * w],
                                                start=(a == 0), stop=(a == 1))
                    last.then_inc(s_pe, 1)

            @block.scalar
            def _(act):
                for c in range(TROWS):
                    act.wait_ge(s_pe, c + 1)
                    nc.scalar.copy(local[:, c * P:(c + 1) * P], ps[:, c % 4, 0:P]).then_inc(s_act, 1)
                for half, (c0, c1) in enumerate(halves):
                    at = slice(c0 * JN * NODE_F, c1 * JN * NODE_F)
                    act.wait_ge(centred, half + 1)
                    nc.scalar.activation(x_s[:, at], x_c[:, at], ACT.Square).then_inc(squared, 1)
                act.wait_ge(s_dve, 12)
                nc.scalar.activation(small[:, 4, :], small[:, 3, :], ACT.Sqrt).then_inc(s_act, 1)
                for n in range(2 * ROWS):
                    act.wait_ge(s_pe, TROWS + n + 1)
                    nc.scalar.activation(x_t[:, n % 2, (n // 2) * P:(n // 2 + 1) * P],
                                         ps[:, 4 + n % 4, 0:P], ACT.Relu).then_inc(s_act, 1)
                act.wait_ge(s_w, 48)
                for b in range(4):
                    w = GPAD // 4
                    act.wait_ge(s_pe, TROWS + 2 * ROWS + b + 1)
                    nc.scalar.activation(node_h[:, b * w:(b + 1) * w], ps[:, b, 0:w], ACT.Relu,
                                         bias=biases[:, 0:1]).then_inc(s_act, 1)
        stage_end()

        need = nc.values_load(counts_i[0:1, 2 * TROWS:2 * TROWS + 1], min_val=1, max_val=LCM * GROUPS)
        n_passes = (need + (LCM - 1)) // LCM
        n_bands = nc.values_load(counts_i[0:1, 2 * TROWS + 1:2 * TROWS + 2], min_val=1, max_val=BANDS)

        def tile_onehot(c):
            return nc.vector.tensor_scalar(onehot[:, c % RING, 0:NGMAX - 1 + BAND], iota_g[:, :],
                                    g0_band[:, c:c + 1], None, ALU.is_equal)

        def band_products(terms, c):
            for n, (g, sums) in enumerate(terms):
                at = NGMAX - 1 - g
                last = nc.tensor.matmul(ps[:, c % 2, 0:BAND], sums, onehot[:, c % RING, at:at + BAND],
                                        start=n == 0, stop=n == len(terms) - 1)
            return last

        def add_band(dve, c, band):
            at = dve.value_load(counts_i[0:1, c:c + 1], min_val=0, max_val=GROUPS - 1) + band * BAND
            return nc.vector.tensor_tensor(agg[:, bass.ds(at, BAND)], agg[:, bass.ds(at, BAND)],
                                           ps[:, c % 2, 0:BAND], ALU.add)

        def next_windows():
            nc.vector.tensor_tensor(g0[:, :], g0[:, :], ngt[:, :], ALU.add)
            for first, end, ng in WINDOWS:
                nc.vector.tensor_scalar(local[:, first * CHUNK:end * CHUNK], local[:, first * CHUNK:end * CHUNK],
                                        float(-JN * ng), None, ALU.add)

        with nc.Fori(0, n_passes) as _p:
            with nc.Block() as block:
                @block.vector
                def _(dve):
                    nc.vector.tensor_copy(local_b, local[:, :]).then_inc(s_dve, 1)
                    dve.wait_ge(s_dve, 1)
                    for w in range(WMAX):
                        n = P * blocks_with(w)
                        nc.vector.tensor_scalar(into[:, w, 0:n], local_b[:, 0:n], float(w), None,
                                                ALU.is_equal).then_inc(s_dve, 1)
                    nc.vector.tensor_copy(g0_band[:, :], g0[:, :])
                    nc.vector.drain()
                    next_windows()
                    dve.wait_ge(s_pe, 1)
                    for c in range(TROWS):
                        w = JN * groups_of_block(c)
                        nc.vector.tensor_tensor(cnt[:, c, 0:w], ps[:, 0, c * WMAX:c * WMAX + w],
                                                valid[:, c * WMAX:c * WMAX + w], ALU.mult)

                @block.tensor
                def _(pe):
                    for w in range(WMAX):
                        pe.wait_ge(s_dve, w + 2)
                        for c in range(blocks_with(w)):
                            last = nc.tensor.matmul(ps[:, 0, c * WMAX + w:c * WMAX + w + 1],
                                                    into[:, w, c * P:(c + 1) * P], ones[:, 0:1],
                                                    start=True, stop=True)
                    last.then_inc(s_pe, 1)
            stage_end()
            with nc.Fori(0, n_bands) as band:
                with nc.Block() as block:
                    @block.scalar
                    def _(act):
                        for c in range(TROWS):
                            if c >= RING:
                                act.wait_ge(s_pe, c - RING + 1)
                            w = JN * groups_of_block(c)
                            nc.scalar.copy(cnt_b[:, c % RING, 0:w * HID].rearrange("p (w o) -> p w o", o=HID),
                                           cnt[:, c, 0:w].unsqueeze(2).to_broadcast([P, w, HID])).then_inc(s_act, 1)

                    @block.vector
                    def _(dve):
                        for c in range(TROWS):
                            if c >= RING:
                                dve.wait_ge(s_pe, c - RING + 1)
                            tile_onehot(c).then_inc(s_dve, 1)
                            if c:
                                dve.wait_ge(s_pe, c)
                                if c >= 2:
                                    dve.wait_ge(s_store, c - 1)
                                add_band(dve, c - 1, band).then_inc(s_store, 1)
                        dve.wait_ge(s_pe, TROWS)
                        dve.wait_ge(s_store, TROWS - 1)
                        add_band(dve, TROWS - 1, band)
                        nc.vector.tensor_scalar(g0_band[:, :], g0_band[:, :], float(-BAND), None, ALU.add)

                    @block.tensor
                    def _(pe):
                        for c in range(TROWS):
                            pe.wait_ge(s_dve, c + 1)
                            pe.wait_ge(s_act, c + 1)
                            if c >= 2:
                                pe.wait_ge(s_store, c - 1)
                            band_products([(g, cnt_b[:, c % RING, g * P:(g + 1) * P])
                                           for g in range(groups_of_block(c))], c).then_inc(s_pe, 1)
                stage_end()
        with nc.Block() as block:
            @block.sync
            def _(sp):
                sp.dma_start(local[:, :], local_dram).then_inc(s_store, 16)
                sp.wait_ge(s_store, 16)

            @block.vector
            def _(dve):
                nc.vector.tensor_scalar(recip[:, :], agg[:, 0:GROUPS], 1.0, None, ALU.max)
                nc.vector.drain()
                nc.vector.reciprocal(recip[:, :], recip[:, :])
        stage_end()

        with nc.Fori(0, LAYERS) as layer:
            h_r = work[:, 0:16 * P].rearrange("p (q w) -> p q w", q=4)
            tab = mk_flat[:, 0:ROWS * JN * ROW_W]
            tab_b = tab.bitcast(BF16).rearrange("p (c j s h) -> p c j s h", c=ROWS, j=JN, s=PARTS)
            quads = [(q * 4, min(4, ROWS - q * 4)) for q in range(-(-ROWS // 4))]
            with nc.Block() as block:
                @block.sync
                def _(sp):
                    for q, (c0, cn) in enumerate(quads):
                        sp.wait_ge(s_dve, 2 * q + 3)
                        sp.dma_start(table_rows[:, c0:c0 + cn, :],
                                     tab.bitcast(U32).rearrange("p (c w) -> p c w", c=ROWS)[:, c0:c0 + cn, :]
                                     ).then_inc(s_store, 16)
                    sp.wait_ge(s_store, 16 * len(quads))

                @block.tensor
                def _(pe):
                    for c in range(ROWS):
                        last = nc.tensor.transpose(ps[:, c // 4, (c % 4) * P:(c % 4 + 1) * P],
                                                   node_h[:, c * P:(c + 1) * P], ident[:, :])
                        if c % 4 == 3 or c == ROWS - 1:
                            last.then_inc(s_pe, 1)

                @block.scalar
                def _(act):
                    for q, (c0, cn) in enumerate(quads):
                        src = ps[:, q, 0:cn * P].rearrange("p (c j h) -> p c j h", c=cn, j=JN)
                        act.wait_ge(s_pe, q + 1)
                        nc.scalar.copy(tab_b[:, c0:c0 + cn, :, 0, :], src).then_inc(s_act, 1)
                        act.wait_ge(s_dve, 2 * q + 2)
                        rest = h_r[:, q, 0:cn * P].rearrange("p (c j h) -> p c j h", c=cn, j=JN)
                        nc.scalar.copy(tab_b[:, c0:c0 + cn, :, 1, :], rest).then_inc(s_act, 1)

                @block.gpsimd
                def _(pool):
                    nc.gpsimd.memset(agg[:, :], 0.0)

                @block.vector
                def _(dve):
                    nc.vector.tensor_copy(g0[:, :], g0_first[:, :]).then_inc(s_dve, 1)
                    for q, (c0, cn) in enumerate(quads):
                        src = ps[:, q, 0:cn * P].rearrange("p (c j h) -> p c j h", c=cn, j=JN)
                        rest = h_r[:, q, 0:cn * P].rearrange("p (c j h) -> p c j h", c=cn, j=JN)
                        dve.wait_ge(s_act, 2 * q + 1)
                        nc.vector.tensor_tensor(rest, src, tab_b[:, c0:c0 + cn, :, 0, :],
                                                ALU.subtract).then_inc(s_dve, 1)
                        dve.wait_ge(s_act, 2 * q + 2)
                        nc.vector.tensor_tensor(tab_b[:, c0:c0 + cn, :, 2, :], rest,
                                                tab_b[:, c0:c0 + cn, :, 1, :], ALU.subtract).then_inc(s_dve, 1)
            stage_end()

            with nc.Fori(0, n_passes) as _p:
                with nc.Block() as block:
                    @block.sync
                    def _(sp):
                        sp.dma_start(ea[0:SUB * EDGE_F, 0, :, :].rearrange("p a e -> p (a e)"),
                                     ea_t[0]).then_inc(ea_in[0], 16)
                        sp.dma_start(w1[:, :], w1_b[bass.ds(layer, 1)].rearrange("a p w -> (a p) w")).then_inc(s_w, 16)
                        sp.dma_start(ea[0:SUB * EDGE_F, 1, :, :].rearrange("p a e -> p (a e)"),
                                     ea_t[1]).then_inc(ea_in[1], 16)
                        sp.dma_start(rootw[:, :],
                                     root_b[bass.ds(layer, 1)].rearrange("a p w -> (a p) w")).then_inc(s_load, 16)
                        sp.dma_start(rootbias[:, :],
                                     root_bias[bass.ds(layer, 1)].rearrange("a p w -> (a p) w")).then_inc(s_load, 16)
                        sp.dma_start(w2[:, :, :].rearrange("p k o -> p (k o)"),
                                     w2_b[bass.ds(layer, 1)].rearrange("a p w -> (a p) w")).then_inc(s_load, 16)
                        with sp.Fori(0, CHUNKS) as i:
                            for s in range(SEGS):
                                sp.wait_ge(xm_done, i * (SEGS * SUBS) + (s * SUBS + 6))
                                sp.dma_start(idx[:, (s + 1) % RING, :],
                                             src_t[bass.ds(i * SEGS + (s + 1), 1)].rearrange("a p t -> (a p) t")
                                             ).then_inc(idx_in[(s + 1) % RING], 16)
                                sp.wait_ge(he_mm, i * SEGS + (s + 1))
                                sp.dma_start(ea[0:SUB * EDGE_F, (s + 2) % RING, :, :].rearrange("p a e -> p (a e)"),
                                             ea_t[bass.ds(i * SEGS + (s + 2), 1)].rearrange("a p w -> (a p) w")
                                             ).then_inc(ea_in[(s + 2) % RING], 16)

                    @block.gpsimd
                    def _(pool):
                        with pool.Fori(0, CHUNKS) as i:
                            for s in range(SEGS):
                                if s:
                                    pool.wait_ge(idx_in[s], i * 16 + 16)
                                else:
                                    pool.wait_ge(idx_in[s], i * 16)
                                for q in range(SUBS):
                                    pool.wait_ge(xm_done, i * (SEGS * SUBS) + (s * SUBS + q + 1))
                                    nc.gpsimd.sem_inc(slot_taken, 1)
                                    for t in range(SUB):
                                        nc.gpsimd.indirect_dma_start(
                                            out=xg[:, s * SUBS + q, t, :], out_offset=None, in_=table,
                                            in_offset=bass.IndirectOffsetOnAxis(
                                                ap=idx[:, s, q * SUB + t:q * SUB + t + 1], axis=0),
                                        ).then_inc(gathered[s * SUBS + q], 16)
                        pool.wait_ge(idx_in[0], CHUNKS * 16)
                        for n in range(GRING):
                            pool.wait_ge(gathered[n], CHUNKS * SUB * 16)

                    def he_rest(slot):
                        nc.vector.tensor_tensor(he_r[:, :, :], he32[:, slot, :, :], hp[:, slot, 0, :, 0:HID],
                                                ALU.subtract).then_inc(he_r1, 1)

                    def he_middle(slot):
                        nc.vector.tensor_copy(hp[:, slot, 1, :, 0:HID], he_r[:, :, :]).then_inc(he_mid, 1)

                    def he_low(slot):
                        nc.vector.tensor_tensor(hp[:, slot, 2, :, 0:HID], he_r[:, :, :],
                                                hp[:, slot, 1, :, 0:HID], ALU.subtract).then_inc(he_split, 1)

                    @block.vector
                    def _(dve):
                        nc.vector.sem_inc(xm_done, SEGS * SUBS)
                        dve.wait_ge(he_act, 1)
                        he_rest(0)
                        dve.wait_ge(he_r1, 1)
                        he_middle(0)
                        dve.wait_ge(he_mid, 1)
                        he_low(0)
                        for first, end, ng in WINDOWS:
                            w = JN * ng
                            with dve.Fori(first, end) as i:
                                for s in range(SEGS):
                                    nc.vector.tensor_tensor(
                                        eq[:, :, 0:w],
                                        local[:, bass.ds(i * CHUNK + s * SEG, SEG)].unsqueeze(2).to_broadcast([P, SEG, w]),
                                        iota_w[:, 0:w].unsqueeze(1).to_broadcast([P, SEG, w]),
                                        ALU.is_equal).then_inc(mask_eq, 1)
                                    dve.wait_ge(mask_eq, i * SEGS + (s + 1))
                                    nc.vector.tensor_scalar(mask[:, s, :, 0:w], eq[:, :, 0:w], -1, None,
                                                            ALU.mult).then_inc(mask_set, 1)
                                    dve.wait_ge(mask_set, i * SEGS + (s + 1))
                                    for q in range(SUBS):
                                        dve.wait_ge(gathered[s * SUBS + q], i * (SUB * 16) + SUB * 16)
                                        dve.wait_ge(units_done, i * (SEGS * SUBS) + (s * SUBS + q + 1))
                                        for a in range(PARTS):
                                            last = nc.vector.tensor_tensor(
                                                xm[:, q, a * SUB * w * PW:(a + 1) * SUB * w * PW].rearrange(
                                                    "p (t w c) -> p t w c", t=SUB, w=w),
                                                xg[:, s * SUBS + q, :, a * PW:(a + 1) * PW].unsqueeze(2).to_broadcast([P, SUB, w, PW]),
                                                mask[:, s, q * SUB:(q + 1) * SUB, 0:w].bitcast(U32).unsqueeze(3).to_broadcast(
                                                    [P, SUB, w, PW]),
                                                ALU.bitwise_and)
                                        last.then_inc(xm_done, 1)
                                        if q == 0:
                                            dve.wait_ge(he_act, i * SEGS + (s + 2))
                                            he_rest((s + 1) % RING)
                                        elif q == 1:
                                            dve.wait_ge(he_r1, i * SEGS + (s + 2))
                                            he_middle((s + 1) % RING)
                                        else:
                                            dve.wait_ge(he_mid, i * SEGS + (s + 2))
                                            he_low((s + 1) % RING)
                        nc.vector.tensor_copy(g0_band[:, :], g0[:, :])
                        nc.vector.drain()
                        next_windows()

                    def he_products(slot):
                        for a in range(SUBS):
                            last = nc.tensor.matmul(he_ps[:, a, 0:SUB * HID], ea[:, slot, a, :], w1[:, :],
                                                    start=True, stop=True)
                        last.then_inc(he_mm, 1)

                    @block.tensor
                    def _(pe):
                        nc.tensor.sem_inc(units_done, SUBS)
                        nc.tensor.sem_inc(he_mm, 1)
                        pe.wait_ge(s_w, 16)
                        for n in range(2):
                            pe.wait_ge(ea_in[n], 16)
                            if n:
                                pe.wait_ge(he_act, n)
                            he_products(n)
                        for first, end, ng in WINDOWS:
                            with pe.Fori(first, end) as i:
                                for s in range(SEGS):
                                    pe.wait_ge(ea_in[(s + 2) % RING], i * 16 + (16 if s == 0 else 32))
                                    pe.wait_ge(he_act, i * SEGS + (s + 2))
                                    if s == 0:
                                        pe.wait_ge(r_done, i + 1)
                                    he_products((s + 2) % RING)
                                    pe.wait_ge(he_split, i * SEGS + (s + 1))
                                    for q in range(SUBS):
                                        pe.wait_ge(xm_done, i * (SEGS * SUBS) + (s * SUBS + q + 10))
                                        pe.wait_ge(evac, i * (SEGS * SUBS) + (s * SUBS + q + 1))
                                        xb = xm[:, q, 0:PARTS * SUB * JN * ng * PW].bitcast(BF16).rearrange(
                                            "p (a u c) -> p a u c", a=PARTS, u=SUB * ng)
                                        for t in range(SUB):
                                            for g in range(ng):
                                                u = (t % 3) * ng + g
                                                for n, (a, b) in enumerate(PRODUCTS):
                                                    last = nc.tensor.matmul(
                                                        ps[:, 2 * q + t // 3, u * K1:(u + 1) * K1],
                                                        xb[:, a, t * ng + g, :], hp[:, s, b, q * SUB + t, :],
                                                        start=n == 0, stop=n == len(PRODUCTS) - 1)
                                        last.then_inc(units_done, 1)
                                pe.wait_ge(evac, i * (SEGS * SUBS) + (SEGS * SUBS + SUBS))
                                pe.wait_ge(s_load, 48)
                                pe.wait_ge(he_act, i * SEGS + (SEGS + 2))
                                for k in range(K1):
                                    last = nc.tensor.matmul(contr[:, 0:CHUNK * ng], w2[:, k, :],
                                                            mk[:, k, 0:CHUNK * ng], start=k == 0, stop=k == K1 - 1)
                                last.then_inc(contr_done, 1)

                    def he_high(slot):
                        he = he_ps[:, :, 0:SUB * HID]
                        nc.scalar.activation(he32[:, slot, :, :].rearrange("p (a t) h -> p a (t h)", a=SUBS), he, ACT.Relu)
                        for a in range(SUBS):
                            last = nc.scalar.activation(hp[:, slot, 0, a * SUB:(a + 1) * SUB, 0:HID],
                                                        he_ps[:, a, 0:SUB * HID].rearrange("p (t h) -> p t h", h=HID),
                                                        ACT.Relu)
                        last.then_inc(he_act, 1)

                    @block.scalar
                    def _(act):
                        nc.scalar.sem_inc(evac, SUBS)
                        nc.scalar.sem_inc(r_done, 1)
                        for n in range(2):
                            act.wait_ge(he_mm, n + 2)
                            he_high(n)
                        for first, end, ng in WINDOWS:
                            with act.Fori(first, end) as i:
                                for s in range(SEGS):
                                    for q in range(SUBS):
                                        n = s * SUBS + q
                                        if q == 0:
                                            act.wait_ge(he_mm, i * SEGS + (s + 4))
                                            act.wait_ge(units_done, i * (SEGS * SUBS) + (s * SUBS + 3))
                                            he_high((s + 2) % RING)
                                        act.wait_ge(units_done, i * (SEGS * SUBS) + (n + 4))
                                        nc.scalar.copy(
                                            mk[:, :, n * SUB * ng:(n + 1) * SUB * ng].rearrange(
                                                "p k (b u) -> p b u k", b=2),
                                            ps[:, 2 * q:2 * q + 2, 0:3 * ng * K1].rearrange(
                                                "p b (u k) -> p b u k", k=K1)).then_inc(evac, 1)
                                act.wait_ge(contr_done, i + 1)
                                nc.scalar.copy(msg_t[:, 0:ng, bass.ds(i * CHUNK, CHUNK)],
                                               contr[:, 0:CHUNK * ng].rearrange("p (t g) -> p g t", g=ng)
                                               ).then_inc(r_done, 1)
                stage_end()

                with nc.Fori(0, n_bands) as band:
                    with nc.Block() as block:
                        @block.tensor
                        def _(pe):
                            def to_rows(c):
                                if c >= RING:
                                    pe.wait_ge(s_load, c - RING + 1)
                                for g in range(groups_of_block(c)):
                                    last = nc.tensor.transpose(ps[:, 4 + c % RING, g * P:(g + 1) * P],
                                                               msg_t[:, g, c * P:(c + 1) * P], ident[:, :])
                                last.then_inc(s_pe, 1)

                            to_rows(0)
                            to_rows(1)
                            for c in range(TROWS):
                                if c + 2 < TROWS:
                                    to_rows(c + 2)
                                pe.wait_ge(s_dve, c + 1)
                                if c >= 2:
                                    pe.wait_ge(s_store, c - 1)
                                band_products([(g, r_parts[:, c % RING, a, g * P:(g + 1) * P])
                                               for g in range(groups_of_block(c)) for a in range(PARTS)],
                                              c).then_inc(s_w, 1)

                        @block.scalar
                        def _(act):
                            def high(c):
                                w = groups_of_block(c) * P
                                act.wait_ge(s_pe, c + 1)
                                if c >= RING:
                                    act.wait_ge(s_w, c - RING + 1)
                                nc.scalar.copy(r_parts[:, c % RING, 0, 0:w],
                                               ps[:, 4 + c % RING, 0:w]).then_inc(s_act, 1)

                            high(0)
                            for c in range(TROWS):
                                if c + 1 < TROWS:
                                    high(c + 1)
                                w = groups_of_block(c) * P
                                act.wait_ge(s_load, c + 1)
                                nc.scalar.copy(r_parts[:, c % RING, 1, 0:w],
                                               r_rest[:, c % RING, 0:w]).then_inc(s_pool, 1)

                        @block.vector
                        def _(dve):
                            def low(c):
                                w = groups_of_block(c) * P
                                dve.wait_ge(s_pool, c + 1)
                                nc.vector.tensor_tensor(r_parts[:, c % RING, 2, 0:w], r_rest[:, c % RING, 0:w],
                                                        r_parts[:, c % RING, 1, 0:w],
                                                        ALU.subtract).then_inc(s_dve, 1)

                            def add(c):
                                dve.wait_ge(s_w, c + 1)
                                if c:
                                    dve.wait_ge(s_store, c)
                                add_band(dve, c, band).then_inc(s_store, 1)

                            for c in range(TROWS):
                                w = groups_of_block(c) * P
                                if c >= RING:
                                    dve.wait_ge(s_w, c - RING + 1)
                                tile_onehot(c)
                                dve.wait_ge(s_act, c + 1)
                                nc.vector.tensor_tensor(r_rest[:, c % RING, 0:w], ps[:, 4 + c % RING, 0:w],
                                                        r_parts[:, c % RING, 0, 0:w],
                                                        ALU.subtract).then_inc(s_load, 1)
                                if c >= 1:
                                    low(c - 1)
                                if c >= 2:
                                    add(c - 2)
                            low(TROWS - 1)
                            add(TROWS - 2)
                            add(TROWS - 1)
                            nc.vector.tensor_scalar(g0_band[:, :], g0_band[:, :], float(-BAND), None, ALU.add)
                    stage_end()

            with nc.Block() as block:
                @block.sync
                def _(sp):
                    sp.dma_start(local[:, :], local_dram).then_inc(s_store, 16)
                    sp.wait_ge(s_store, 16)

                @block.tensor
                def _(pe):
                    for b, (g_at, g_n) in enumerate(GBANKS):
                        nc.tensor.matmul(ps[:, b, 0:g_n], rootw[:, :], node_h[:, g_at:g_at + g_n],
                                         start=True, stop=True).then_inc(s_pe, 1)

                @block.vector
                def _(dve):
                    nc.vector.tensor_tensor(agg[:, 0:GROUPS], agg[:, 0:GROUPS], recip[:, :], ALU.mult)
                    nc.vector.drain()
                    for b, (g_at, g_n) in enumerate(GBANKS):
                        dve.wait_ge(s_pe, b + 1)
                        nc.vector.tensor_tensor(agg[:, g_at:g_at + g_n], agg[:, g_at:g_at + g_n],
                                                ps[:, b, 0:g_n], ALU.add).then_inc(s_dve, 1)

                @block.scalar
                def _(act):
                    for b, (g_at, g_n) in enumerate(GBANKS):
                        act.wait_ge(s_dve, b + 1)
                        act.wait_ge(s_pe, b + 1)
                        nc.scalar.activation(node_h[:, g_at:g_at + g_n], agg[:, g_at:g_at + g_n], ACT.Relu,
                                             bias=rootbias[:, 0:1])
            stage_end()

        z_t = work[:, 0:GPAD]
        d_t = work[:, GPAD:2 * GPAD]
        x_res = work[:, 2 * GPAD:2 * GPAD + XW].rearrange("p (c w) -> p c w", c=ROWS)
        y = mk_flat[:, 0:XW].rearrange("p (c w) -> p c w", c=ROWS)
        wout = mk_flat[:, XW:XW + JN * LAT]
        wdec1 = mk_flat[:, XW + 64:XW + 64 + P]
        wdec2 = mk_flat[:, XW + 192:XW + 192 + JN * NODE_F]
        bdec2 = mk_flat[:, XW + 448:XW + 448 + JN * NODE_F]
        FW = GPAD // 4
        with nc.Block() as block:
            @block.sync
            def _(sp):
                sp.dma_start(wout, lout_b).then_inc(s_w, 16)
                sp.dma_start(biases[0:JN * LAT, 1:2], lout_bias).then_inc(s_w, 16)
                sp.dma_start(wdec1[0:JN * LAT, :], dec1_b).then_inc(s_w, 16)
                sp.dma_start(biases[:, 2:3], dec1_bias).then_inc(s_w, 16)
                sp.dma_start(wdec2, dec2_b).then_inc(s_w, 16)
                sp.dma_start(bdec2, dec2_bias).then_inc(s_w, 16)
                sp.dma_start(x_res, x_rows).then_inc(s_load, 16)
                sp.wait_ge(s_dve, ROWS + 1)
                sp.dma_start(out, y).then_inc(s_store, 16)
                sp.wait_ge(s_store, 16)

            @block.tensor
            def _(pe):
                pe.wait_ge(s_w, 96)
                for b in range(4):
                    nc.tensor.matmul(ps[0:JN * LAT, b, 0:FW], wout, node_h[:, b * FW:(b + 1) * FW],
                                     start=True, stop=True).then_inc(s_pe, 1)
                for b in range(4):
                    pe.wait_ge(s_act, b + 1)
                    nc.tensor.matmul(ps[:, 4 + b, 0:FW], wdec1[0:JN * LAT, :],
                                     z_t[0:JN * LAT, b * FW:(b + 1) * FW],
                                     start=True, stop=True).then_inc(s_pe, 1)
                pe.wait_ge(s_act, 8)
                for c in range(ROWS):
                    if c >= 4:
                        pe.wait_ge(s_dve, 1 + c - 3)
                    nc.tensor.matmul(ps[:, c % 4, 0:JN * NODE_F], d_t[:, c * P:(c + 1) * P], wdec2,
                                     start=True, stop=True).then_inc(s_pe, 1)

            @block.scalar
            def _(act):
                act.wait_ge(s_w, 96)
                for b in range(4):
                    act.wait_ge(s_pe, b + 1)
                    nc.scalar.activation(z_t[0:JN * LAT, b * FW:(b + 1) * FW], ps[0:JN * LAT, b, 0:FW],
                                         ACT.Identity, bias=biases[0:JN * LAT, 1:2]).then_inc(s_act, 1)
                for b in range(4):
                    act.wait_ge(s_pe, 4 + b + 1)
                    nc.scalar.activation(d_t[:, b * FW:(b + 1) * FW], ps[:, 4 + b, 0:FW], ACT.Relu,
                                         bias=biases[:, 2:3]).then_inc(s_act, 1)

            @block.vector
            def _(dve):
                dve.wait_ge(s_w, 96)
                dve.wait_ge(s_load, 16)
                nc.vector.tensor_tensor(x_res, x_res, bdec2.unsqueeze(1).to_broadcast([P, ROWS, JN * NODE_F]),
                                        ALU.add).then_inc(s_dve, 1)
                dve.wait_ge(s_dve, 1)
                for c in range(ROWS):
                    dve.wait_ge(s_pe, 8 + c + 1)
                    nc.vector.tensor_tensor(y[:, c, :], ps[:, c % 4, 0:JN * NODE_F], x_res[:, c, :],
                                            ALU.add).then_inc(s_dve, 1)


def kernel(**inputs):
    import numpy as np

    import concourse.bacc as bacc
    from concourse.bass_utils import run_bass_kernel_spmd

    a = {k.replace("L0_gnn_", ""): np.asarray(v) for k, v in inputs.items()}

    def diagonal(w, n):
        *lead, r, c = w.shape
        m = np.zeros((*lead, n * r, n * c), w.dtype)
        for j in range(n):
            m[..., j * r:(j + 1) * r, j * c:(j + 1) * c] = w
        return m

    def padded(x, n, fill=0):
        return np.concatenate([x, np.full((n - x.shape[0], *x.shape[1:]), fill, x.dtype)])

    def by_row(x):
        return np.ascontiguousarray(x)

    x = padded(a["x"], GPAD * JN)
    x_rows = by_row(x.reshape(ROWS, P, JN * NODE_F).transpose(1, 0, 2))

    def tiles(x, fill=0):
        return padded(x, TILES * P, fill).reshape(TILES, P, *x.shape[1:])[::-1]

    src = tiles(a["src"]).reshape(CHUNKS * SEGS, SEG, P)
    src_t = by_row(np.concatenate([src, src[:1]]).transpose(0, 2, 1))
    dst_t = by_row(padded(tiles(a["dst"], -1), TPAD, -1).reshape(TROWS, P, P).transpose(1, 0, 2).reshape(P, TPAD))
    ea = padded(tiles(a["edge_attr_16"]), HE_SEGS * SEG).reshape(HE_SEGS, SUBS, SUB, P, EDGE_F)
    ea_t = by_row(ea.transpose(0, 2, 4, 1, 3).reshape(HE_SEGS, SUB * EDGE_F, SUBS * P))

    w1_b = np.concatenate([diagonal(a["edge_w1"], SUB), np.tile(a["edge_b1"], SUB)[:, None, :]], 1)
    w2 = np.concatenate([a["edge_w2"], a["edge_b2"][:, None, :]], 1).reshape(LAYERS, K1, HID, HID)
    w2_b = by_row(diagonal(w2, JN).transpose(0, 2, 1, 3).reshape(LAYERS, P, K1 * P))
    root_b = diagonal(a["root_w"], JN)
    root_bias = np.tile(a["root_b"], JN)[:, :, None]
    lin_w = np.zeros((P, 2, P), a["lin_in_w"].dtype)
    for h in range(2):
        lin_w[:, h, h * 2 * HID:(h + 1) * 2 * HID] = diagonal(a["lin_in_w"], 2)

    tile_groups = np.array([groups_of_tile(t) for t in range(TPAD)], np.float32).reshape(TROWS, P).T
    window = np.arange(WMAX)[None, None, :] < JN * tile_groups[:, :, None]
    arrays = {
        "x_rows": x_rows, "src_t": src_t, "dst_t": dst_t, "ea_t": ea_t, "w1_b": w1_b, "w2_b": w2_b,
        "root_b": root_b, "root_bias": root_bias, "lin_w": lin_w,
        "lin_bias": np.tile(a["lin_in_b"], JN)[:, None],
        "lout_b": diagonal(a["lin_out_w"], JN), "lout_bias": np.tile(a["lin_out_b"], JN)[:, None],
        "dec1_b": diagonal(a["dec_w1"], JN), "dec1_bias": np.tile(a["dec_b1"], JN)[:, None],
        "dec2_b": diagonal(a["dec_w2"], JN), "dec2_bias": np.tile(a["dec_b2"], (P, JN)),
        "tile_ng": tile_groups, "tile_valid": window.reshape(P, TROWS * WMAX).astype(np.float32),
        "tile_scale": LCM / tile_groups,
    }
    arrays = {k: np.ascontiguousarray(v) for k, v in arrays.items()}
    nc = bacc.Bacc("TRN2", target_bir_lowering=False, num_devices=1)
    aps = {k: nc.dram_tensor(k, v.shape, mybir.dt.from_np(v.dtype), kind="ExternalInput").ap()
           for k, v in arrays.items()}
    aps["src_t"] = aps["src_t"].bitcast(U32)
    out = nc.dram_tensor("out_rows", (P, ROWS, JN * NODE_F), F32, kind="ExternalOutput").ap()
    gnn_program(nc, **aps, out=out)
    r = run_bass_kernel_spmd(nc, [arrays], core_ids=[0])
    rows = np.asarray(r.results[0]["out_rows"])
    return rows.transpose(1, 0, 2).reshape(GPAD * JN, NODE_F)[:N_NODES]
```
